# Optimizing a Trainium2 kernel written in Bass

```python
import numpy as np
import jax
import jax.numpy as jnp

def _softmax(x, axis=-1):
    return jax.nn.softmax(x, axis=axis)

def _gelu(x):
    return jax.nn.gelu(x, approximate=True)

def _silu(x):
    return jax.nn.silu(x)

def _sigmoid(x):
    return jax.nn.sigmoid(x)

def _layernorm(x, axis=-1, eps=1e-05):
    m = jnp.mean(x, axis=axis, keepdims=True)
    v = jnp.var(x, axis=axis, keepdims=True)
    return (x - m) / jnp.sqrt(v + eps)

def _scatter_add(tgt, idx, src, axis=0):
    return tgt.at[idx].add(src)

def _segment_sum(src, seg, n):
    return jax.ops.segment_sum(src, seg, n)
kernel_name = 'mk_decoder_preln_d1_seqx_r4_f5f559'

def setup_inputs(seed: int=0):
    np.random.seed(seed)
    _w = jnp.asarray

    def _rec_inputs():
        import jax
        import jax.numpy as jnp
        _rk = jax.random.key(seed)
        x = 7.22e-05 + 1 * jax.random.normal(jax.random.fold_in(_rk, 1), (4, 512, 512), jnp.float32)
        _lenS = 512 - jax.random.randint(jax.random.fold_in(_rk, 7), (4,), 0, max(1, 512 // 4) + 1, jnp.int32)
        _lenS2 = 512 - jax.random.randint(jax.random.fold_in(_rk, 8), (4,), 0, max(1, 512 // 4) + 1, jnp.int32)
        _ctx_2048P = jax.random.normal(jax.random.fold_in(_rk, 11), (4, 16, 512), jnp.float32)
        _ctx_2048c = jax.random.dirichlet(jax.random.fold_in(_rk, 511), 0.3 * jnp.ones((16,), jnp.float32), (4, 512))
        _ctx_2048t = jnp.einsum('bsk,bkd->bsd', _ctx_2048c, _ctx_2048P)
        _ctx_2048t = _ctx_2048t * jax.lax.rsqrt(jnp.mean(jnp.square(_ctx_2048t)) + 1e-12) * 0.953939
        ctx_2048 = 4.13588e-05 + 0.999923 * (_ctx_2048t + 0.3 * jax.random.normal(jax.random.fold_in(_rk, 611), (4, 512, 512), jnp.float32))
        return (x, ctx_2048)
    x, ctx_2048 = _rec_inputs()

    def _L0_attn_setup():
        import jax, jax.numpy as jnp
        import numpy as np
        import math
        N_Q = 128
        N_K = 128
        N_V = 128
        D_MODEL = 512
        N_HEADS = 16
        B, T = (8, 1024)
        key = jax.random.key(seed)
        ks = jax.random.split(key, 9)
        s = 0.02
        return {'x': jax.random.normal(ks[0], (B, T, D_MODEL), dtype=jnp.float32), 'Wq': jax.random.normal(ks[1], (D_MODEL, N_Q * N_HEADS), dtype=jnp.float32) * s, 'bq': jnp.zeros((N_Q * N_HEADS,), dtype=jnp.float32), 'Wk': jax.random.normal(ks[2], (D_MODEL, N_K * N_HEADS), dtype=jnp.float32) * s, 'bk': jnp.zeros((N_K * N_HEADS,), dtype=jnp.float32), 'Wv': jax.random.normal(ks[3], (D_MODEL, N_V * N_HEADS), dtype=jnp.float32) * s, 'bv': jnp.zeros((N_V * N_HEADS,), dtype=jnp.float32), 'Wo': jax.random.normal(ks[4], (N_V * N_HEADS, D_MODEL), dtype=jnp.float32) * s, 'bo': jnp.zeros((D_MODEL,), dtype=jnp.float32)}
    _L0_attn_all = _L0_attn_setup()
    _L0_attn_in = {k: v for k, v in _L0_attn_all.items() if k in ('Wq', 'bq', 'Wk', 'bk', 'Wv', 'bv', 'Wo', 'bo')}
    del _L0_attn_all

    def _L0_xattn_setup():
        import jax, jax.numpy as jnp
        import numpy as np
        N_HEAD = 8
        key = jax.random.key(seed)
        k1, k2, k3 = jax.random.split(key, 3)
        B, D, L = (4, 256, 512)
        q = jax.random.normal(k1, (B, D, L), dtype=jnp.float32)
        k = jax.random.normal(k2, (B, D, L), dtype=jnp.float32)
        v = jax.random.normal(k3, (B, D, L), dtype=jnp.float32)
        gamma = jnp.ones((), dtype=jnp.float32)
        return {'q': q, 'k': k, 'v': v, 'gamma': gamma}
    _L0_xattn_all = _L0_xattn_setup()
    _L0_xattn_in = {k: v for k, v in _L0_xattn_all.items() if k in ('gamma',)}
    del _L0_xattn_all

    def _L0_ffn_setup():
        import jax, jax.numpy as jnp
        import numpy as np
        D_MODEL = 512
        HIDDEN = int(2 * D_MODEL * 4 / 3)

        def ternary_quant(w):
            s = jnp.mean(jnp.abs(w))
            q = jnp.clip(jnp.round(w / s), -1.0, 1.0) * s
            return w + jax.lax.stop_gradient(q - w)
        key = jax.random.key(seed)
        k0, k1, k2, k3 = jax.random.split(key, 4)
        x = jax.random.normal(k0, (4, 1024, D_MODEL), dtype=jnp.float32)
        std_in = 1.0 / np.sqrt(D_MODEL)
        std_h = 1.0 / np.sqrt(HIDDEN)
        w1 = jax.random.uniform(k1, (HIDDEN, D_MODEL), jnp.float32, -std_in, std_in)
        w3 = jax.random.uniform(k2, (HIDDEN, D_MODEL), jnp.float32, -std_in, std_in)
        w2 = jax.random.uniform(k3, (D_MODEL, HIDDEN), jnp.float32, -std_h, std_h)
        return {'x': x, 'w1': w1, 'w3': w3, 'w2': w2}
    _L0_ffn_all = _L0_ffn_setup()
    _L0_ffn_in = {k: v for k, v in _L0_ffn_all.items() if k in ('w1', 'w3', 'w2')}
    del _L0_ffn_all
    return {'x': x, 'ctx_2048': ctx_2048, 'L0_attn_Wq': _L0_attn_in['Wq'], 'L0_attn_bq': _L0_attn_in['bq'], 'L0_attn_Wk': _L0_attn_in['Wk'], 'L0_attn_bk': _L0_attn_in['bk'], 'L0_attn_Wv': _L0_attn_in['Wv'], 'L0_attn_bv': _L0_attn_in['bv'], 'L0_attn_Wo': _L0_attn_in['Wo'], 'L0_attn_bo': _L0_attn_in['bo'], 'L0_xattn_gamma': _L0_xattn_in['gamma'], 'L0_ffn_w1': _L0_ffn_in['w1'], 'L0_ffn_w3': _L0_ffn_in['w3'], 'L0_ffn_w2': _L0_ffn_in['w2']}

def reference(x, ctx_2048, L0_attn_Wq, L0_attn_bq, L0_attn_Wk, L0_attn_bk, L0_attn_Wv, L0_attn_bv, L0_attn_Wo, L0_attn_bo, L0_xattn_gamma, L0_ffn_w1, L0_ffn_w3, L0_ffn_w2):
    import jax
    import jax.numpy as jnp

    def _L0_attn_ref(x, Wq, bq, Wk, bk, Wv, bv, Wo, bo):
        import jax, jax.numpy as jnp
        import numpy as np
        import math
        N_Q = 128
        N_K = 128
        N_V = 128
        D_MODEL = 512
        N_HEADS = 16
        B, T = (8, 1024)
        Bx, Tx, _ = x.shape
        q = (x @ Wq + bq).reshape(Bx, Tx, N_Q, N_HEADS)
        k = (x @ Wk + bk).reshape(Bx, Tx, N_K, N_HEADS)
        v = (x @ Wv + bv).reshape(Bx, Tx, N_V, N_HEADS)
        q = jnp.transpose(q, (0, 3, 2, 1))
        k = jnp.transpose(k, (0, 3, 1, 2))
        v = jnp.transpose(v, (0, 3, 2, 1))
        att = jax.nn.softmax(q @ k / math.sqrt(N_K), axis=-1)
        y = att @ v
        y = jnp.transpose(y, (0, 2, 1, 3)).reshape(Bx, -1, N_V * N_HEADS)
        return y @ Wo + bo

    def _L0_xattn_ref(q, k, v, gamma):
        import jax, jax.numpy as jnp
        import numpy as np
        N_HEAD = 8
        B, Dq, Lq = q.shape
        Dv, Lk = (v.shape[-2], v.shape[-1])
        h = N_HEAD
        dq = Dq // h
        dv = Dv // h
        qh = q.reshape(B, h, dq, Lq)
        kh = k.reshape(B, h, dq, Lk)
        vh = v.reshape(B, h, dv, Lk)
        scale = 1.0 / jnp.sqrt(jnp.asarray(dq, dtype=q.dtype))
        qk = jnp.einsum('bhdq,bhdl->bhql', qh, kh) * scale
        sm = jax.nn.softmax(qk, axis=-1)
        ret = jnp.einsum('bhql,bhdl->bhdq', sm, vh)
        ret = ret.reshape(B, Dv, Lq)
        return gamma * ret

    def _L0_ffn_ref(x, w1, w3, w2):
        import jax, jax.numpy as jnp
        import numpy as np
        D_MODEL = 512
        HIDDEN = int(2 * D_MODEL * 4 / 3)

        def ternary_quant(w):
            s = jnp.mean(jnp.abs(w))
            q = jnp.clip(jnp.round(w / s), -1.0, 1.0) * s
            return w + jax.lax.stop_gradient(q - w)
        w1q = ternary_quant(w1)
        w3q = ternary_quant(w3)
        w2q = ternary_quant(w2)
        h1 = jnp.einsum('bsd,hd->bsh', x, w1q)
        h3 = jnp.einsum('bsd,hd->bsh', x, w3q)
        g = jax.nn.silu(h1) * h3
        return jnp.einsum('bsh,dh->bsd', g, w2q)
    x = x + _L0_attn_ref(_layernorm(x, axis=-1), L0_attn_Wq, L0_attn_bq, L0_attn_Wk, L0_attn_bk, L0_attn_Wv, L0_attn_bv, L0_attn_Wo, L0_attn_bo)
    x = x + _L0_xattn_ref(_layernorm(x, axis=-1), ctx_2048, ctx_2048, L0_xattn_gamma)
    x = x + _L0_ffn_ref(_layernorm(x, axis=-1), L0_ffn_w1, L0_ffn_w3, L0_ffn_w2)
    return x

_drawn_inputs = setup_inputs


def setup_inputs(seed=0):
    import zlib

    import numpy as np

    out = dict(_drawn_inputs(seed))
    spreads = {'L0_attn_bq': (0.0, 0.388),
     'L0_attn_bk': (0.0, 0.385),
     'L0_attn_bv': (0.0, 0.8),
     'L0_attn_bo': (0.0, 0.1)}
    factors = {}
    for name, (base, spread) in spreads.items():
        noise = np.random.default_rng([zlib.crc32(name.encode()), seed]).standard_normal(out[name].shape)
        drawn = base * np.exp(spread * noise) if base else spread * noise
        out[name] = jnp.asarray(drawn.astype(out[name].dtype))
    for name, factor in factors.items():
        out[name] = (out[name] * factor).astype(out[name].dtype)
    return out
```

```python
from contextlib import ExitStack

import concourse.bass as bass
from concourse import mybir

F32 = mybir.dt.float32
F32R = mybir.dt.float32r
I32 = mybir.dt.int32
ACT = mybir.ActivationFunctionType
ALU = mybir.AluOpType
AX = mybir.AxisListType.X

P = 128
B, T, C = 4, 512, 512
CK = C // P
TJ = T // P
NH, HG = 16, 4
GROUPS = NH // HG
PB = 2
PASSES = B // PB
EPS = 1e-5
SCALE_A = float(P) ** -0.5
XH, XD = 8, 64
SCALE_X = float(XD) ** -0.5
HID = int(2 * C * 4 / 3)
HC = -(-HID // P)
HP = HC * P
SHIFT = 0.125

WP = 105
WS = HID * C // WP // GROUPS
assert WP * WS * GROUPS == HID * C
RING_A, RING_B, RING_C = 4, 2, 2
A_TILES = PB * CK + 2 * GROUPS * PB * CK
B_TILES = PB * CK + GROUPS * PB * CK
C_TILES = 4 * GROUPS + GROUPS * PB * HG
MV = 2 * GROUPS * PB * CK
W_LOADS = 2 * GROUPS
TANH_LAG, GATE_LAG = 1, 2


def newton_rsqrt(dve, link, y, tmp, v):
    link(dve.tensor_scalar(v, v, EPS, None, ALU.add))
    link(dve.tensor_scalar(tmp.bitcast(I32), v.bitcast(I32), 1, None, ALU.logical_shift_right))
    link(dve.tensor_scalar(y.bitcast(I32), tmp.bitcast(I32), -1.0, float(0x5F3759DF), ALU.mult, ALU.add))
    for _ in range(4):
        link(dve.tensor_tensor(tmp, y, y, ALU.mult))
        link(dve.tensor_tensor(tmp, tmp, v, ALU.mult))
        link(dve.tensor_scalar(tmp, tmp, -0.5, 1.5, ALU.mult, ALU.add))
        link(dve.tensor_tensor(y, y, tmp, ALU.mult))


def three_passes(pe, out, wh, wl, xh, xl, start, stop):
    pe.matmul(out, wh, xh, start=start, stop=False)
    pe.matmul(out, wh, xl, start=False, stop=False)
    return pe.matmul(out, wl, xh, start=False, stop=stop)


def decoder_block(nc, x, ctx, wa, wb, wq_t, bq_col, bkv, bo, gamma, w1t, w3t, w2t, out):
    x1_dram = nc.dram_tensor("x1_scratch", [B, T, C], F32, kind="Internal").ap()
    stat_dram = nc.dram_tensor("stat_scratch", [B, T, 2], F32, kind="Internal").ap()
    beta_dram = nc.dram_tensor("beta_scratch", [W_LOADS, HG * P], F32, kind="Internal").ap()
    wq_dram = [nc.dram_tensor(f"ternary_scratch{w}", list(v.shape), F32, kind="Internal").ap()
               for w, v in enumerate((w1t, w3t, w2t))]
    w_flat = [v.rearrange("a b -> (a b)").rearrange("(p n) -> p n", p=WP) for v in (w1t, w3t, w2t)]
    wq_flat = [v.rearrange("a b -> (a b)").rearrange("(p n) -> p n", p=WP) for v in wq_dram]
    stack = ExitStack()
    with stack:
        def sem(name):
            return stack.enter_context(nc.semaphore(name))

        s = {}
        for name in (
            "ident", "x_in0", "x_in1", "bo_in", "bq_in", "raw_a", "raw_b", "bkv_in", "colsum", "beta_col", "beta_out", "link",
            "xn", "xh", "ph", "xl", "pl", "xacc_bo", "xth", "xtl", "shat", "gzh",
            "a_ready", "a_free", "b_ready", "b_free", "c_ready", "c_free",
            "wah", "wal", "wbh", "wbl", "beta_add", "tmp", "mvh", "mvl",
            "mx", "nmx", "rinv", "pn", "pth", "ptl", "x1_ready", "x1_out", "zero_beta",
            "const_in", "w_raw", "w_abs", "w_sum", "w_thr", "w_q", "w_scale", "w_pad", "w_low", "w_stored", "gam",
            "x1d_in0", "x1d_in1", "kd_in0", "kd_in1", "gam_in", "w_in", "x2_in", "x2_kept", "r_half", "u0_ready", "u1_ready", "u0_free", "u1_free", "gh2", "gl2", "y_ready", "st_in", "xq", "qh", "ql", "kh", "kl", "vth", "vtl", "x2",
            "s_ready", "s_free", "t_ready", "t_free", "r_ready", "r_free", "f_ready", "f_free",
            "xmx", "xnmx", "xrinv", "xpn", "pxh", "pxl", "r_sum", "x3n", "x3h", "x3l", "link_b",
            "tanh", "gate_sp", "gate_dve", "gate_pool", "u", "g", "gh", "gl", "y", "y_out",
        ):
            s[name] = sem("s_" + name)
        ident = stack.enter_context(nc.sbuf_tensor("ident", [P, P], F32))
        wsum = stack.enter_context(nc.sbuf_tensor("wsum", [P, 3, GROUPS], F32))
        wmean = stack.enter_context(nc.sbuf_tensor("wmean", [P, 3], F32))
        wthr = stack.enter_context(nc.sbuf_tensor("wthr", [P, 2, 3], F32))
        wscale = stack.enter_context(nc.sbuf_tensor("wscale", [P, 1], F32))
        bank = [stack.enter_context(nc.psum_tensor(f"bank{i}", [P, 512], F32)) for i in range(8)]

        CREDIT = {"dve": ("y", "u0_free", "u1_free", "w_q"), "act": ("w_abs",), "pool": ("gl2",), "sp": ("w_stored", "y_out")}

        def credit(eng, name):
            for c in CREDIT[name]:
                eng.sem_inc(s[c], 1)

        def gate(eng, name):
            eng.sem_inc(s["gate_" + name], 1)

        mem_a = ExitStack()

        def sa(name, shape, dt=F32):
            return mem_a.enter_context(nc.sbuf_tensor(name, shape, dt))

        mem_w = ExitStack()
        wraw = mem_w.enter_context(nc.sbuf_tensor("wraw", [WP, 3, WS], F32))
        wlow = mem_w.enter_context(nc.sbuf_tensor("wlow", [WP, WS], F32))
        mem_w.close()
        gh, gl = sa("gh", [P, PB, CK, C], F32R), sa("gl", [P, PB, CK, C], F32R)
        xth, xtl = sa("xth", [P, PB, CK, T], F32R), sa("xtl", [P, PB, CK, T], F32R)
        wah, wal = sa("wah", [P, CK, 512], F32R), sa("wal", [P, CK, 512], F32R)
        wbh, wbl = sa("wbh", [P, CK, 512], F32R), sa("wbl", [P, CK, 512], F32R)
        raw_a, raw_b = sa("raw_a", [P, CK, 512]), sa("raw_b", [P, CK, 512])
        work = sa("work", [P, 16, 512], F32R)
        xh, xl, ph, pl = (work[:, 4 * i:4 * i + 4, :] for i in range(4))
        mh = work[:, 0:8, :].rearrange("p (k b) n -> p k b n", b=PB)
        ml = work[:, 8:16, :].rearrange("p (k b) n -> p k b n", b=PB)
        vh, vl, zh, zl = xh, xl, ph, pl
        xnf = sa("xnf", [P, TJ, C])
        tmp = sa("tmp", [P, 2, 512])
        ptf = sa("ptf", [P, GROUPS, 2, 512])
        pth, ptl = sa("pth", [P, 2, 512], F32R), sa("ptl", [P, 2, 512], F32R)
        pw = sa("pw", [P, 2, 512])
        xacc = sa("xacc", [P, PB, TJ, C])
        beta_bc, bkv_bc, bo_bc = sa("beta_bc", [P, 512]), sa("bkv_bc", [P, 512]), sa("bo_bc", [P, C])
        bqc, cs, betac = sa("bqc", [P, NH]), sa("cs", [P, NH]), sa("betac", [P, NH])
        shat = sa("shat", [P, PB, CK])
        bst = sa("bst", [P, TJ, 6])
        mvar = sa("mvar", [P, TJ, 2])
        rstd, ntmp, nvar = sa("rstd", [P, TJ]), sa("ntmp", [P, TJ]), sa("nvar", [P, TJ])
        stat = sa("stat", [P, PB, TJ, 2])
        mx, nmx = sa("mx", [P, 2, 4]), sa("nmx", [P, 2, 4])
        rs, rinv = sa("rs", [P, 2, 4]), sa("rinv", [P, 2, 4])
        mem_a.close()

        def a_bank(u):
            return bank[u % RING_A]

        def b_bank(u):
            return bank[RING_A + u % RING_B]

        def c_bank(u):
            return bank[RING_A + RING_B + u % RING_C]

        def a_xt(p, u):
            return A_TILES * p + u

        def a_m(p, g, u):
            return g * 8 + (A_TILES * p + PB * CK + u)

        def a_v(p, g, u):
            return g * 8 + (A_TILES * p + PB * CK + GROUPS * 8 + u)

        def b_g(p, u):
            return B_TILES * p + u

        def b_z(p, g, u):
            return g * 8 + (B_TILES * p + PB * CK + u)

        def c_s(p, g, pr):
            return g * 4 + (C_TILES * p + pr)

        def c_t(p, g, pr):
            return g * 4 + (C_TILES * p + 2 + pr)

        def c_out(p, g, u):
            return g * 8 + (C_TILES * p + 4 * GROUPS + u)

        def mv_m(p, g, u):
            return g * 8 + (MV * p + u)

        def mv_v(p, g, u):
            return g * 8 + (MV * p + GROUPS * 8 + u)

        def load_of(p, k):
            return k + W_LOADS * p

        def wait_bank(eng, free, index, ring):
            if isinstance(index, int) and index < ring:
                return
            eng.wait_ge(s[free], index - (ring - 1))

        def last_step(p, k):
            return p == PASSES - 1 and isinstance(k, int) and k == W_LOADS - 1


        mem_b = ExitStack()

        def sb(name, shape, dt=F32):
            return mem_b.enter_context(nc.sbuf_tensor(name, shape, dt))

        w13 = sb("w13", [P, 2, CK, HID], F32R)
        w2 = sb("w2", [P, HC, C], F32R)
        gth, gtl = sb("gth", [P, HC, T], F32R), sb("gtl", [P, HC, T], F32R)
        x3h, x3l = sb("x3h", [P, CK, T], F32R), sb("x3l", [P, CK, T], F32R)
        pxh, pxl = sb("pxh", [P, CK, C], F32R), sb("pxl", [P, CK, C], F32R)
        pe_x = sb("pe_x", [P, 4, C])
        x1d = sb("x1d", [P, 2, C])
        kd = sb("kd", [P, 2, C])
        qst = sb("qst", [P, 2, C], F32R)
        kh, kl = sb("kh", [P, 2, C], F32R), sb("kl", [P, 2, C], F32R)
        vts = sb("vts", [P, 4, CK, P], F32R)
        x2 = sb("x2", [P, TJ, C])
        x2res = sb("x2res", [P, TJ, C])
        th, uu, gf = sb("th", [P, T]), sb("uu", [P, T]), sb("gf", [P, T])
        stx = sb("stx", [P, XH, 2])
        xmx, xrs, xri = sb("xmx", [P, 4]), sb("xrs", [P, 4]), sb("xri", [P, 4])
        gam = sb("gam", [P, 1])
        bst_b, mv_b = sb("bst_b", [P, TJ, 6]), sb("mv_b", [P, TJ, 2])
        rstd_b, ntmp_b, nvar_b = sb("rstd_b", [P, TJ]), sb("ntmp_b", [P, TJ]), sb("nvar_b", [P, TJ])
        mem_b.close()
        s_bank, t_bank, r_bank, u_bank = bank[0:2], bank[2:4], bank[4], bank[5:7]
        y_bank = [bank[7], bank[5]]

        S_TILES = 4 * XH
        T_TILES = XH + 4 * XH + TJ
        U_PIECES = 2 * HC
        LINK_B = 2 + 1 + 19

        def t_v(b, h):
            return b * T_TILES + (5 * h - 4 if h else 0)

        def t_p(b, h, q):
            return b * T_TILES + (5 * (h + 1) - 3 + q if h < XH - 1 else 5 * XH - 4 + q)

        def t_x3(b, t):
            return b * T_TILES + (XH + 4 * XH + t)

        def pieces(n):
            if n < 0 or n >= S_TILES:
                return range(0)
            return range(U_PIECES * n // S_TILES, U_PIECES * (n + 1) // S_TILES)

        def chunk_rows(i):
            return min(P, HID - P * i)

        def turns(engine_loop, body):
            body(0, None)
            with engine_loop(1, B) as b:
                body(b, b - 1)
            body(None, B - 1)

        def rows(t, b):
            return t[b] if isinstance(b, int) else t[bass.ds(b, 1)].rearrange("a t c -> (a t) c")

        def sp_head(sp, b, h):
            slot, n = h % 2, b * XH + h
            if h >= 2 or not isinstance(b, int) or b > 0:
                sp.wait_ge(s["ql"], n - 1)
                gate(sp, "sp")
                sp.wait_ge(s["t_ready"], t_v(b, h - 2) + 1 if h >= 2 else t_v(b - 1, XH - 2 + h) + 1)
            for half in range(2):
                part = slice(XD * half, XD * (half + 1))
                sp.dma_start(x1d[part, slot, :], rows(x1_dram, b)[XD * h:XD * (h + 1), :]).then_inc(s[f"x1d_in{slot}"], 16)
                sp.dma_start(kd[part, slot, :], rows(ctx, b)[XD * h:XD * (h + 1), :]).then_inc(s[f"kd_in{slot}"], 16)

        def sp_stats(sp, b):
            if not isinstance(b, int) or b > 0:
                sp.wait_ge(s["xq"], b * XH)
            for half in range(2):
                sp.dma_start(stx[XD * half:XD * (half + 1)], rows(stat_dram, b).rearrange("(h p) c -> p h c", p=XD)).then_inc(s["st_in"], 16)

        def sp_rows(sp, b, f):
            if b is not None:
                sp_stats(sp, b)
                sp_head(sp, b, 0)
                sp_head(sp, b, 1)
            if f is not None:
                for t in range(TJ):
                    sp.wait_ge(s["y"], 1 + f * TJ + (t + 1))
                    sp.dma_start(rows(out, f)[t * P:(t + 1) * P, :], x2res[:, t, :]).then_inc(s["y_out"], 16)
            if b is not None:
                if not isinstance(b, int) or b > 0:
                    sp.wait_ge(s["x2_kept"], b * TJ)
                sp.dma_start(x2[:], rows(x1_dram, b).rearrange("(t p) c -> p t c", p=P)).then_inc(s["x2_in"], 16)
                for h in range(2, XH):
                    sp_head(sp, b, h)

        def stage_b_sp(sp):
            sp.wait_ge(s["x1_out"], 32 * B)
            sp.wait_ge(s["w_stored"], 1 + 48 * GROUPS)
            sp.dma_start(gam[:], gamma.to_broadcast([P, 1])).then_inc(s["gam_in"], 16)
            sp_rows(sp, 0, None)
            for w in range(2):
                sp.dma_start(w13[:, w].bitcast(F32), wq_dram[w].rearrange("(c p) n -> p c n", p=P)).then_inc(s["w_in"], 16)
            full = HC - 1
            sp.dma_start(w2[:, 0:full, :].bitcast(F32), wq_dram[2][0:full * P, :].rearrange("(c p) n -> p c n", p=P)).then_inc(s["w_in"], 16)
            sp.dma_start(w2[0:chunk_rows(full), full, :].bitcast(F32), wq_dram[2][full * P:HID, :]).then_inc(s["w_in"], 16)
            sp_rows(sp, 1, None)
            with sp.Fori(2, B) as b:
                sp_rows(sp, b, b - 2)
            sp_rows(sp, None, B - 2)
            sp_rows(sp, None, B - 1)
            sp.wait_ge(s["y_out"], 1 + 16 * TJ * B)
            sp.wait_ge(s["gate_dve"], B)
            sp.wait_ge(s["gate_pool"], B * S_TILES)
            sp.wait_ge(s["gate_sp"], 1)

        def pe_vt(pe, b, h):
            pe.wait_ge(s[f"kd_in{h % 2}"], b * 128 + 32 * (h // 2 + 1))
            pe_wait(pe, "t_free", t_v(b, h), 2)
            tb = t_bank[(5 * h - 4 if h else 0) % 2]
            for c in range(CK):
                mm = pe.transpose(tb[:, c * P:(c + 1) * P], kd[:, h % 2, c * P:(c + 1) * P], ident[:])
            mm.then_inc(s["t_ready"], 1)

        def pe_wait(pe, free, index, ring):
            if not isinstance(index, int) or index >= ring:
                pe.wait_ge(s[free], index - (ring - 1))

        def pe_pt(pe, b, h, q):
            pe.wait_ge(s["xpn"], b * S_TILES + (4 * h + q + 1))
            pe_wait(pe, "t_free", t_p(b, h, q), 2)
            tb = t_bank[t_p(0, h, q) % 2]
            for c in range(CK):
                mm = pe.transpose(tb[:, c * P:(c + 1) * P], pe_x[:, q, c * P:(c + 1) * P], ident[:])
            mm.then_inc(s["t_ready"], 1)

        def pe_sx(pe, b, h, q):
            if q == 0:
                pe.wait_ge(s["ql"], b * XH + (h + 1))
                pe.wait_ge(s["kl"], b * XH + (h + 1))
            pe_wait(pe, "s_free", b * S_TILES + (4 * h + q), 2)
            lhs = qst[:, h % 2, q * P:(q + 1) * P]
            pe.matmul(s_bank[q % 2][:], lhs, kh[:, h % 2, :], start=True, stop=False)
            pe.matmul(s_bank[q % 2][:], lhs, kl[:, h % 2, :], start=False, stop=True).then_inc(s["s_ready"], 1)

        def pe_ret(pe, b, h, half):
            n = b * XH + h
            pe.wait_ge(s["t_free"], t_p(b, h, 2 * half + 1) + 1)
            if half == 0:
                pe_wait(pe, "r_free", n, 1)
            cols = slice(2 * P * half, 2 * P * (half + 1))
            for c in range(CK):
                lhs = vts[:, h % 4, c, :]
                pe.matmul(r_bank[:, cols], lhs, pxh[:, c, cols], start=c == 0, stop=False)
                mm = pe.matmul(r_bank[:, cols], lhs, pxl[:, c, cols], start=False, stop=c == CK - 1)
            mm.then_inc(s["r_ready"], 1)

        def pe_up(pe, f, piece):
            i, w = piece // 2, piece % 2
            m = chunk_rows(i)
            if piece == 0:
                pe.wait_ge(s["t_free"], t_x3(f, TJ))
                pe.wait_ge(s["y"], 1 + f * TJ)
            pe.wait_ge(s[f"u{w}_free"], 1 + f * HC + i)
            for c in range(CK):
                lhs = w13[:, w, c, i * P:i * P + m]
                pe.matmul(u_bank[w][0:m, :], lhs, x3h[:, c, :], start=c == 0, stop=False)
                mm = pe.matmul(u_bank[w][0:m, :], lhs, x3l[:, c, :], start=False, stop=c == CK - 1)
            mm.then_inc(s[f"u{w}_ready"], 1)

        def pe_down(pe, f, t):
            pe.wait_ge(s["gl2"], 1 + f * HC + HC)
            if t >= 2:
                pe.wait_ge(s["y"], 1 + f * TJ + (t - 1))
            if t == 1:
                pe.wait_ge(s["u0_free"], 1 + f * HC + HC)
            for i in range(HC):
                k = chunk_rows(i)
                pe.matmul(y_bank[t % 2][:], gth[0:k, i, t * P:(t + 1) * P], w2[0:k, i, :], start=i == 0, stop=False)
                mm = pe.matmul(y_bank[t % 2][:], gtl[0:k, i, t * P:(t + 1) * P], w2[0:k, i, :], start=False, stop=i == HC - 1)
            mm.then_inc(s["y_ready"], 1)

        def pe_x3(pe, b, t):
            pe.wait_ge(s["x3n"], b * TJ + (t + 1))
            pe_wait(pe, "t_free", t_x3(b, t), 2)
            tb = t_bank[t_x3(0, t) % 2]
            for c in range(CK):
                mm = pe.transpose(tb[:, c * P:(c + 1) * P], pe_x[:, t, c * P:(c + 1) * P], ident[:])
            mm.then_inc(s["t_ready"], 1)

        def pe_turn(pe, b, f):
            for h in range(XH):
                for q in range(4):
                    if b is not None:
                        if q == 0:
                            pe_vt(pe, b, h)
                        pe_sx(pe, b, h, q)
                        if q == 1 and h >= 2:
                            pe_ret(pe, b, h - 2, 1)
                        if q == 3 and h >= 1:
                            pe_ret(pe, b, h - 1, 0)
                        if h:
                            pe_pt(pe, b, h - 1, q)
                    if f is not None:
                        for piece in pieces(4 * h + q):
                            pe_up(pe, f, piece)
            if b is not None:
                pe_pt(pe, b, XH - 1, 0)
                pe_ret(pe, b, XH - 2, 1)
                for q in range(1, 4):
                    pe_pt(pe, b, XH - 1, q)
            if f is not None:
                pe_down(pe, f, 0)
            if b is not None:
                pe_ret(pe, b, XH - 1, 0)
                pe_ret(pe, b, XH - 1, 1)
            if f is not None:
                for t in range(1, TJ - 1):
                    pe_down(pe, f, t)
            if b is not None:
                pe_x3(pe, b, 0)
                pe_x3(pe, b, 1)
            if f is not None:
                pe_down(pe, f, TJ - 1)
            if b is not None:
                for t in range(2, TJ):
                    pe_x3(pe, b, t)

        def stage_b_pe(pe):
            pe.wait_ge(s["x1_out"], 32 * B)
            pe_turn(pe, 0, None)
            pe.wait_ge(s["w_in"], 64)
            with pe.Fori(1, B) as b:
                pe_turn(pe, b, b - 1)
            pe_turn(pe, None, B - 1)

        def act_prep(act, b, h):
            n, slot = b * XH + h, h % 2
            act.wait_ge(s[f"kd_in{slot}"], b * 128 + 32 * (h // 2 + 1))
            if h >= 2 or not isinstance(b, int) or b > 0:
                act.wait_ge(s["s_ready"], b * S_TILES + 4 * (h - 1))
            act.activation(kh[:, slot, :], kd[:, slot, :], ACT.Copy).then_inc(s["kh"], 1)
            act.wait_ge(s["xq"], n + 1)
            act.activation(qst[:, slot, :], x1d[:, slot, :], ACT.Copy).then_inc(s["qh"], 1)

        def act_vt(act, b, h):
            tb = t_bank[(5 * h - 4 if h else 0) % 2][:].rearrange("p (c n) -> p c n", n=P)
            act.wait_ge(s["t_ready"], t_v(b, h) + 1)
            act.activation(vts[:, h % 4, :, 0:XD], tb[:, :, 0:XD], ACT.Copy).then_inc(s["vth"], 1)

        def act_px(act, b, h, q):
            tb = t_bank[t_p(0, h, q) % 2][:].rearrange("p (c n) -> p c n", n=P)
            act.wait_ge(s["t_ready"], t_p(b, h, q) + 1)
            act.activation(pxh[:, :, q * P:(q + 1) * P], tb, ACT.Copy).then_inc(s["pxh"], 1)

        def act_exp(act, b, h, q):
            act.wait_ge(s["xmx"], b * S_TILES + (4 * h + q + 1))
            act.activation(pe_x[:, q, :], s_bank[q % 2][:], ACT.Exp, bias=xmx[:, q:q + 1],
                           accum_out=xrs[:, q:q + 1]).then_inc(s["s_free"], 1)

        def act_tanh(act, f, piece):
            i, w = piece // 2, piece % 2
            m = chunk_rows(i)
            n = f * HC + i
            if w == 0:
                act.wait_ge(s["u0_ready"], n + 1)
                act.wait_ge(s["u0_free"], 1 + n)
                act.activation(th[0:m, :], u_bank[0][0:m, :], ACT.Tanh, scale=wthr[0:m, 0, 0:1]).then_inc(s["tanh"], 1)

        def act_gate(act, f, piece):
            i, w = piece // 2, piece % 2
            m = chunk_rows(i)
            if w:
                act.wait_ge(s["u1_free"], 1 + f * HC + i + 1)
                act.activation(gth[0:m, i, :], gf[0:m, :], ACT.Copy).then_inc(s["gh2"], 1)

        def act_keep(act, f, t):
            act.wait_ge(s["x3n"], (f + 1) * TJ)
            act.wait_ge(s["y_out"], 1 + f * (16 * TJ))
            act.activation(x2res[:, t, :], x2[:, t, :], ACT.Copy).then_inc(s["x2_kept"], 1)

        def act_turn(act, b, f):
            if b is not None:
                act_prep(act, b, 0)
            for n in range(S_TILES):
                h, q = n // 4, n % 4
                if f is not None:
                    for piece in pieces(n - TANH_LAG):
                        act_tanh(act, f, piece)
                if b is not None:
                    if q == 0:
                        act_vt(act, b, h)
                    if h:
                        act_px(act, b, h - 1, q)
                    act_exp(act, b, h, q)
                    if q == 0 and h + 1 < XH:
                        act_prep(act, b, h + 1)
                if f is not None:
                    if n < TJ:
                        act_keep(act, f, n)
                    for piece in pieces(n - GATE_LAG):
                        act_gate(act, f, piece)
            if f is not None:
                for n in range(S_TILES, S_TILES + GATE_LAG):
                    for piece in pieces(n - TANH_LAG):
                        act_tanh(act, f, piece)
                    for piece in pieces(n - GATE_LAG):
                        act_gate(act, f, piece)
            if b is not None:
                for q in range(4):
                    act_px(act, b, XH - 1, q)
                for t in range(TJ):
                    tb = t_bank[t_x3(0, t) % 2][:].rearrange("p (c n) -> p c n", n=P)
                    act.wait_ge(s["t_ready"], t_x3(b, t) + 1)
                    act.activation(x3h[:, :, t * P:(t + 1) * P], tb, ACT.Copy).then_inc(s["x3h"], 1)

        def stage_b_act(act):
            act.wait_ge(s["x1_out"], 32 * B)
            turns(act.Fori, lambda b, f: act_turn(act, b, f))

        def dve_q(dve, b, h):
            n, slot = b * XH + h, h % 2
            dve.wait_ge(s[f"x1d_in{slot}"], b * 128 + 32 * (h // 2 + 1))
            if h == 0:
                dve.wait_ge(s["st_in"], b * 32 + 32)
            dve.tensor_scalar(x1d[:, slot, :], x1d[:, slot, :], stx[:, h, 0:1], stx[:, h, 1:2],
                              ALU.subtract, ALU.mult).then_inc(s["xq"], 1)

        def dve_vt(dve, b, h):
            tb = t_bank[(5 * h - 4 if h else 0) % 2][:].rearrange("p (c n) -> p c n", n=P)
            dve.wait_ge(s["vth"], b * XH + (h + 1))
            dve.tensor_tensor(vts[:, h % 4, :, XD:P], tb[:, :, XD:P], vts[:, h % 4, :, 0:XD].bitcast(F32),
                              ALU.subtract).then_inc(s["t_free"], 1)

        def dve_px(dve, b, h, q):
            tb = t_bank[t_p(0, h, q) % 2][:].rearrange("p (c n) -> p c n", n=P)
            dve.wait_ge(s["pxh"], b * S_TILES + (4 * h + q + 1))
            dve.tensor_tensor(pxl[:, :, q * P:(q + 1) * P], tb, pxh[:, :, q * P:(q + 1) * P].bitcast(F32),
                              ALU.subtract).then_inc(s["t_free"], 1)

        def dve_max(dve, b, h, q):
            dve.wait_ge(s["s_ready"], b * S_TILES + (4 * h + q + 1))
            dve.reduce_max(xmx[:, q:q + 1], s_bank[q % 2][:], axis=AX, negate=True).then_inc(s["xmx"], 1)

        def dve_rinv(dve, b, h, q):
            dve.wait_ge(s["s_free"], b * S_TILES + (4 * h + q + 1))
            dve.reciprocal(xri[:, q:q + 1], xrs[:, q:q + 1]).then_inc(s["xrinv"], 1)

        def dve_ret(dve, b, h):
            n = b * XH + h
            rows_ = slice(XD * (h % 2), XD * (h % 2) + XD)
            dve.wait_ge(s["r_ready"], 2 * n + 2)
            dst = x2[rows_, h // 2, :]
            if h == 0:
                dve.wait_ge(s["x2_in"], b * 16 + 16)
            dve.tensor_tensor(dst, dst, r_bank[0:XD, :], ALU.add).then_inc(s["r_half"], 1)
            dve.wait_ge(s["r_half"], n + 1)
            dve.tensor_tensor(dst, dst, r_bank[XD:P, :], ALU.add).then_inc(s["r_free"], 1)

        def dve_moments(dve, b, t):
            dve.wait_ge(s["r_free"], b * XH + 2 * (t + 1))
            dve.bn_stats(bst_b[:, t, :], x2[:, t, :])

        def dve_up(dve, f, piece):
            i, w = piece // 2, piece % 2
            m = chunk_rows(i)
            n = f * HC + i
            if w == 0:
                dve.wait_ge(s["tanh"], n + 1)
                dve.wait_ge(s["u1_free"], 1 + n)
                dve.scalar_tensor_tensor(uu[0:m, :], th[0:m, :], 1.0, u_bank[0][0:m, :], ALU.add, ALU.mult).then_inc(s["u0_free"], 1)
            else:
                dve.wait_ge(s["u1_ready"], n + 1)
                dve.wait_ge(s["u0_free"], 1 + n + 1)
                dve.wait_ge(s["gl2"], 1 + n)
                dve.scalar_tensor_tensor(gf[0:m, :], uu[0:m, :], wscale[0:m, 0:1], u_bank[1][0:m, :], ALU.mult, ALU.mult).then_inc(s["u1_free"], 1)

        def dve_y(dve, f, t):
            dve.wait_ge(s["y_ready"], f * TJ + (t + 1))
            if t == 0:
                dve.wait_ge(s["x2_kept"], f * TJ + TJ)
            dve.scalar_tensor_tensor(x2res[:, t, :], y_bank[t % 2][:], wmean[:, 2:3], x2res[:, t, :],
                                     ALU.mult, ALU.add).then_inc(s["y"], 1)

        def dve_x3(dve, b, count):
            def link(ins):
                count[0] += 1
                ins.then_inc(s["link_b"], 1)
                dve.wait_ge(s["link_b"], b * LINK_B + count[0])
            dve.wait_ge(s["r_free"], b * XH + XH)
            for t in range(TJ - 1, TJ):
                i = dve.bn_stats(bst_b[:, t, :], x2[:, t, :])
            link(i)
            gate(dve, "dve")
            for t in range(TJ):
                i = dve.bn_aggr(mv_b[:, t, :], bst_b[:, t, :])
            link(i)
            link(dve.tensor_copy(nvar_b[:], mv_b[:, :, 1]))
            newton_rsqrt(dve, link, rstd_b[:], ntmp_b[:], nvar_b[:])
            assert count[0] == LINK_B, count

        def dve_x3n(dve, b, t):
            dve.wait_ge(s["t_ready"], t_x3(b, 0))
            dve.tensor_scalar(pe_x[:, t, :], x2[:, t, :], mv_b[:, t, 0:1], rstd_b[:, t:t + 1], ALU.subtract, ALU.mult).then_inc(s["x3n"], 1)

        def dve_x3l(dve, b, t):
            tb = t_bank[t_x3(0, t) % 2][:].rearrange("p (c n) -> p c n", n=P)
            dve.wait_ge(s["x3h"], b * TJ + (t + 1))
            dve.tensor_tensor(x3l[:, :, t * P:(t + 1) * P], tb, x3h[:, :, t * P:(t + 1) * P].bitcast(F32),
                              ALU.subtract).then_inc(s["t_free"], 1)

        def dve_turn(dve, b, f):
            if b is not None:
                dve_q(dve, b, 0)
            for n in range(S_TILES):
                h, q = n // 4, n % 4
                if b is not None:
                    if q == 0:
                        dve_vt(dve, b, h)
                    if q == 2 and h >= 2:
                        dve_ret(dve, b, h - 2)
                    dve_max(dve, b, h, q)
                if f is not None:
                    for piece in pieces(n - TANH_LAG):
                        dve_up(dve, f, piece)
                if b is not None:
                    if h:
                        dve_px(dve, b, h - 1, q)
                    if n:
                        dve_rinv(dve, b, (n - 1) // 4, (n - 1) % 4)
                    if q == 0 and h + 1 < XH:
                        dve_q(dve, b, h + 1)
                    if q == 0 and h >= 4 and h % 2 == 0:
                        dve_moments(dve, b, (h - 4) // 2)
            if f is not None:
                for n in range(S_TILES, S_TILES + TANH_LAG):
                    for piece in pieces(n - TANH_LAG):
                        dve_up(dve, f, piece)
            if b is not None:
                dve_rinv(dve, b, XH - 1, 3)
                dve_px(dve, b, XH - 1, 0)
                dve_ret(dve, b, XH - 2)
                for q in range(1, 4):
                    dve_px(dve, b, XH - 1, q)
                dve_moments(dve, b, TJ - 2)
            if f is not None:
                dve_y(dve, f, 0)
            if b is not None:
                dve_ret(dve, b, XH - 1)
                dve_x3(dve, b, [0])
                for t in range(TJ):
                    dve_x3n(dve, b, t)
            if f is not None:
                for t in range(1, TJ - 1):
                    dve_y(dve, f, t)
            if b is not None:
                dve_x3l(dve, b, 0)
                dve_x3l(dve, b, 1)
            if f is not None:
                dve_y(dve, f, TJ - 1)
            if b is not None:
                for t in range(2, TJ):
                    dve_x3l(dve, b, t)

        def stage_b_dve(dve):
            dve.wait_ge(s["x1_out"], 32 * B)
            turns(dve.Fori, lambda b, f: dve_turn(dve, b, f))

        def pool_prep(pool, b, h):
            n, slot = b * XH + h, h % 2
            pool.wait_ge(s["kh"], n + 1)
            pool.tensor_tensor(kl[:, slot, :], kd[:, slot, :], kh[:, slot, :].bitcast(F32), ALU.subtract).then_inc(s["kl"], 1)
            pool.wait_ge(s["qh"], n + 1)
            pool.wait_ge(s["kl"], n + 1)
            pool.tensor_tensor(qst[XD:P, slot, :], x1d[XD:P, slot, :], qst[XD:P, slot, :].bitcast(F32), ALU.subtract).then_inc(s["ql"], 1)
            pool.wait_ge(s["ql"], n + 1)

        def pool_prob(pool, b, h, q):
            pool.wait_ge(s["xrinv"], b * S_TILES + (4 * h + q + 1))
            gate(pool, "pool")
            pool.tensor_scalar(pe_x[:, q, :], pe_x[:, q, :], xri[:, q:q + 1], gam[:], ALU.mult, ALU.mult).then_inc(s["xpn"], 1)

        def pool_up(pool, f, piece):
            i, w = piece // 2, piece % 2
            if w:
                m = chunk_rows(i)
                pool.wait_ge(s["gh2"], f * HC + (i + 1))
                pool.tensor_tensor(gtl[0:m, i, :], gf[0:m, :], gth[0:m, i, :].bitcast(F32), ALU.subtract).then_inc(s["gl2"], 1)

        def pool_turn(pool, b, f):
            if b is not None:
                pool_prep(pool, b, 0)
            for n in range(S_TILES):
                h, q = n // 4, n % 4
                if b is not None:
                    if n:
                        pool_prob(pool, b, (n - 1) // 4, (n - 1) % 4)
                    if q == 0 and h + 1 < XH:
                        pool_prep(pool, b, h + 1)
                if f is not None:
                    for piece in pieces(n - GATE_LAG):
                        pool_up(pool, f, piece)
            if b is not None:
                pool_prob(pool, b, XH - 1, 3)
            if f is not None:
                for n in range(S_TILES, S_TILES + GATE_LAG):
                    for piece in pieces(n - GATE_LAG):
                        pool_up(pool, f, piece)

        def stage_b_pool(pool):
            pool.wait_ge(s["x1_out"], 32 * B)
            pool.wait_ge(s["gam_in"], 16)
            turns(pool.Fori, lambda b, f: pool_turn(pool, b, f))

        def sp_raw_b(sp, p, k):
            sp.wait_ge(s["wbl"], CK * load_of(p, k))
            sp.dma_start(raw_b[:], wb[bass.ds(k, 1)].rearrange("a (c p) n -> (a p) c n", p=P)
                         if not isinstance(k, int) else wb[k].rearrange("(c p) n -> p c n", p=P)
                         ).then_inc(s["raw_b"], 16)

        def sp_raw_a(sp, p, k):
            sp.wait_ge(s["wal"], CK * load_of(p, k))
            if isinstance(k, int):
                src, brow = wa[k].rearrange("(c p) n -> p c n", p=P), beta_dram[k:k + 1, :]
            else:
                src = wa[bass.ds(k, 1)].rearrange("a (c p) n -> (a p) c n", p=P)
                brow = beta_dram[bass.ds(k, 1), :]
            sp.dma_start(raw_a[:], src).then_inc(s["raw_a"], 16)
            sp.dma_start(beta_bc[:], brow.to_broadcast([P, 512])).then_inc(s["raw_a"], 16)

        def sp_bkv(sp, p, k):
            sp.wait_ge(s["tmp"], 8 * load_of(p, k))
            row = bkv[k:k + 1, :] if isinstance(k, int) else bkv[bass.ds(k, 1), :]
            sp.dma_start(bkv_bc[:], row.to_broadcast([P, 512])).then_inc(s["bkv_in"], 16)

        def sp_step(sp, p, k):
            sp_raw_b(sp, p, k)
            sp_raw_a(sp, p, k)
            sp_bkv(sp, p, k)

        def sp_weights(sp, p, g):
            sp.wait_ge(s["a_ready"], a_m(p, GROUPS - 1, 8))
            if p == 0:
                sp.wait_ge(s["w_abs"], 1 + g * 3)
            else:
                sp.wait_ge(s["w_q"], 1 + g * 3)
                gate(sp, "sp")
                sp.wait_ge(s["w_stored"], 1 + g * 48)
            for w in range(3):
                sp.dma_start(wraw[:, w, :], w_flat[w][:, bass.ds(g * WS, WS)]).then_inc(s["w_raw"], 16)
            if p == 1:
                for w in range(3):
                    sp.wait_ge(s["w_q"], 1 + g * 3 + (w + 1))
                    sp.dma_start(wq_flat[w][:, bass.ds(g * WS, WS)], wraw[:, w, :]).then_inc(s["w_stored"], 16)

        def sp_x(sp, b):
            if b >= PB:
                sp.wait_ge(s["x1_out"], 32 * (b - PB + 1))
            sp.dma_start(xacc[:, b % PB], x[b].rearrange("(p j) c -> p j c", j=TJ)).then_inc(s[f"x_in{b % PB}"], 16)

        def sp_x1_store(sp, p, i):
            b = PB * p + i
            sp.wait_ge(s["x1_ready"], b + 1)
            sp.dma_start(x1_dram[b].rearrange("(p j) c -> p j c", j=TJ), xacc[:, i]).then_inc(s["x1_out"], 16)
            sp.dma_start(stat_dram[b].rearrange("(p j) c -> p j c", j=TJ), stat[:, i]).then_inc(s["x1_out"], 16)

        block = stack.enter_context(nc.Block())

        @block.sync
        def _(sp):
            credit(sp, "sp")
            sp_x(sp, 0)
            sp_x(sp, 1)
            sp.dma_start(bqc[:], bq_col).then_inc(s["bq_in"], 16)
            sp.dma_start(bo_bc[:], bo.rearrange("(a n) -> a n", a=1).to_broadcast([P, C])).then_inc(s["bo_in"], 16)
            for g in range(GROUPS):
                if g:
                    sp.wait_ge(s["colsum"], g)
                sp.dma_start(raw_a[:], wq_t[g]).then_inc(s["raw_a"], 16)
            sp_raw_b(sp, 0, 0)
            sp.wait_ge(s["colsum"], GROUPS)
            sp.wait_ge(s["beta_col"], 1)
            with nc.allow_non_contiguous_dma(reason="2048 words once"):
                sp.dma_start(beta_dram[0:GROUPS, :].rearrange("g (h n) -> n (g h)", n=P), betac[:]).then_inc(s["beta_out"], 16)
            sp.wait_ge(s["zero_beta"], 1)
            for g in range(GROUPS):
                sp.dma_start(beta_dram[GROUPS + g:GROUPS + g + 1, :], pw[0:1, 0, :]).then_inc(s["beta_out"], 16)
            sp.wait_ge(s["beta_out"], 16 * (GROUPS + 1))
            sp_raw_a(sp, 0, 0)
            sp_bkv(sp, 0, 0)
            for p in range(PASSES):
                with sp.Fori(1, GROUPS + 1) as k:
                    sp_step(sp, p, k)
                with sp.Fori(0, GROUPS - 1) as g:
                    sp_step(sp, p, g + GROUPS + 1)
                    sp_weights(sp, p, g)
                sp_weights(sp, p, GROUPS - 1)
                if p < PASSES - 1:
                    sp_step_next = p + 1
                    sp_raw_b(sp, sp_step_next, 0)
                    sp_raw_a(sp, sp_step_next, 0)
                    sp_bkv(sp, sp_step_next, 0)
                for i in range(PB):
                    sp_x1_store(sp, p, i)
                    if p < PASSES - 1:
                        sp_x(sp, PB * (p + 1) + i)
            stage_b_sp(sp)

        def pe_norm(pe, p):
            for i in range(PB):
                n = PB * TJ * p + TJ * i
                pe.wait_ge(s["xn"], n + TJ)
                for c in range(CK):
                    u = CK * i + c
                    wait_bank(pe, "a_free", a_xt(p, u), RING_A)
                    for j in range(TJ):
                        mm = pe.transpose(a_bank(u)[:, j * P:(j + 1) * P], xnf[:, j, c * P:(c + 1) * P], ident[:])
                    mm.then_inc(s["a_ready"], 1)
                for c in range(CK):
                    u = CK * i + c
                    wait_bank(pe, "b_free", b_g(p, u), RING_B)
                    for j in range(TJ):
                        if c == 0:
                            pe.wait_ge(s["xl"], n + j + 1)
                            pe.wait_ge(s["pl"], n + j + 1)
                        mm = three_passes(pe, b_bank(u)[:], xh[:, j, c * P:(c + 1) * P], xl[:, j, c * P:(c + 1) * P],
                                          ph[:, j, :], pl[:, j, :], j == 0, j == TJ - 1)
                    mm.then_inc(s["b_ready"], 1)

        def pe_m(pe, p, g):
            for u in range(PB * CK):
                i, c = u // CK, u % CK
                if c == 0 and isinstance(g, int):
                    pe.wait_ge(s["gzh"], b_g(p, CK * (i + 1)))
                    pe.wait_ge(s["b_free"], b_g(p, CK * (i + 1)))
                wait_bank(pe, "a_free", a_m(p, g, u), RING_A)
                for k in range(CK):
                    if u == 0:
                        pe.wait_ge(s["wbl"], load_of(p, g) * CK + (k + 1))
                    mm = three_passes(pe, a_bank(u)[:], gh[:, i, k, c * P:(c + 1) * P], gl[:, i, k, c * P:(c + 1) * P],
                                      wbh[:, k, :], wbl[:, k, :], k == 0, k == CK - 1)
                mm.then_inc(s["a_ready"], 1)

        def pe_t(pe, p, g):
            for pr in range(2):
                pe.wait_ge(s["pn"], (g * 2) + (2 * GROUPS * p + pr + 1))
                pe.wait_ge(s["c_free"], c_t(p, g, pr) - (RING_C - 1))
                for q in range(4):
                    mm = pe.transpose(c_bank(pr)[:, q * P:(q + 1) * P], pw[:, pr, q * P:(q + 1) * P], ident[:])
                mm.then_inc(s["c_ready"], 1)

        def pe_s(pe, p, g):
            pe.wait_ge(s["wal"], load_of(p, g) * CK + CK)
            pe.wait_ge(s["mvl"], mv_m(p, g, 8))
            for pr in range(2):
                wait_bank(pe, "c_free", c_s(p, g, pr), RING_C)
                for h in range(2):
                    col = (2 * pr + h) * P
                    for k in range(CK):
                        mm = three_passes(pe, c_bank(pr)[:, 256 * h:256 * (h + 1)],
                                          wah[:, k, col:col + P], wal[:, k, col:col + P],
                                          mh[:, k, :, col:col + P], ml[:, k, :, col:col + P], k == 0, k == CK - 1)
                mm.then_inc(s["c_ready"], 1)

        def pe_v(pe, p, g, i):
            if i == 0:
                pe.wait_ge(s["xth"], PB * CK * (p + 1))
                pe.wait_ge(s["xtl"], PB * CK * (p + 1))
            for j in range(TJ):
                u = TJ * i + j
                wait_bank(pe, "a_free", a_v(p, g, u), RING_A)
                for k in range(CK):
                    if u == 0:
                        pe.wait_ge(s["wal"], load_of(p, g + GROUPS) * CK + (k + 1))
                    mm = three_passes(pe, a_bank(u)[:], xth[:, i, k, j * P:(j + 1) * P], xtl[:, i, k, j * P:(j + 1) * P],
                                      wah[:, k, :], wal[:, k, :], k == 0, k == CK - 1)
                mm.then_inc(s["a_ready"], 1)

        def pe_z(pe, p, g, i):
            for h in range(HG):
                u = HG * i + h
                wait_bank(pe, "b_free", b_z(p, g, u), RING_B)
                for j in range(TJ):
                    if h == 0:
                        pe.wait_ge(s["mvl"], mv_v(p, g, TJ * i + j + 1))
                        if i == 0:
                            pe.wait_ge(s["wbl"], load_of(p, g + GROUPS) * CK + (j + 1))
                    mm = three_passes(pe, b_bank(u)[:], vh[:, j, h * P:(h + 1) * P], vl[:, j, h * P:(h + 1) * P],
                                      wbh[:, j, :], wbl[:, j, :], j == 0, j == TJ - 1)
                mm.then_inc(s["b_ready"], 1)

        def pe_out(pe, p, g, i):
            if i == 0:
                pe.wait_ge(s["ptl"], g + (GROUPS * p + 1))
            for h in range(HG):
                u = HG * i + h
                pe.wait_ge(s["gzh"], b_z(p, g, u + 1))
                pe.wait_ge(s["b_free"], b_z(p, g, u + 1))
                pe.wait_ge(s["c_free"], c_out(p, g, u) - (RING_C - 1))
                q = (h % 2 * PB + i) * P
                mm = three_passes(pe, c_bank(u)[:], pth[:, h // 2, q:q + P], ptl[:, h // 2, q:q + P],
                                  zh[:, h, :], zl[:, h, :], True, True)
                mm.then_inc(s["c_ready"], 1)

        def pe_values(pe, p, g):
            pe_v(pe, p, g, 0)
            pe_z(pe, p, g, 0)
            pe_v(pe, p, g, 1)
            pe_out(pe, p, g, 0)
            pe_z(pe, p, g, 1)
            pe_out(pe, p, g, 1)

        @block.tensor
        def _(pe):
            pe.wait_ge(s["ident"], 2)
            for p in range(PASSES):
                pe_norm(pe, p)
                pe_m(pe, p, 0)
                pe_s(pe, p, 0)
                with pe.Fori(1, GROUPS) as g:
                    pe_m(pe, p, g)
                    pe_t(pe, p, g - 1)
                    pe_s(pe, p, g)
                pe_t(pe, p, GROUPS - 1)
                with pe.Fori(0, GROUPS - 1) as g:
                    pe_values(pe, p, g)
                pe_values(pe, p, GROUPS - 1)
            stage_b_pe(pe)

        def act_norm(act, p):
            for i in range(PB):
                n = PB * TJ * p + TJ * i
                if i:
                    act.wait_ge(s["b_ready"], b_g(p, CK))
                elif p:
                    act.wait_ge(s["w_abs"], 1 + 3 * GROUPS)
                for j in range(TJ):
                    act.wait_ge(s["xn"], n + j + 1)
                    act.activation(xh[:, j, :], xnf[:, j, :], ACT.Copy).then_inc(s["xh"], 1)
                    act.activation(ph[:, j, :], xnf[:, j, :], ACT.Copy, bias=SHIFT).then_inc(s["ph"], 1)
                for c in range(CK):
                    u = CK * i + c
                    act.wait_ge(s["a_ready"], a_xt(p, u) + 1)
                    act.activation(xth[:, i, c, :], a_bank(u)[:], ACT.Copy).then_inc(s["xth"], 1)
                for c in range(CK):
                    u = CK * i + c
                    act.wait_ge(s["b_ready"], b_g(p, u) + 1)
                    act.activation(gh[:, i, c, :], b_bank(u)[:], ACT.Copy).then_inc(s["gzh"], 1)

        def act_split_b(act, p, k, used, count):
            if used:
                act.wait_ge(s[used], count)
            act.wait_ge(s["raw_b"], load_of(p, k) * 16 + 16)
            for c in range(CK):
                act.activation(wbh[:, c, :], raw_b[:, c, :], ACT.Copy).then_inc(s["wbh"], 1)

        def act_split_a(act, p, k, used, count):
            if used:
                act.wait_ge(s[used], count)
            for c in range(CK):
                act.wait_ge(s["beta_add"], load_of(p, k) * CK + (c + 1))
                act.activation(wah[:, c, :], raw_a[:, c, :], ACT.Copy).then_inc(s["wah"], 1)

        def act_scores(act, p, g, first):
            for u in range(8):
                i, c = u // CK, u % CK
                act.wait_ge(s["tmp"], mv_m(p, g, u + 1))
                if u == 0:
                    act.wait_ge(s["a_ready"], a_m(p, g, 1))
                act.activation(mh[:, c, i, :], tmp[:, u % 2, :], ACT.Copy).then_inc(s["mvh"], 1)
            act_split_b(act, p, g + 1, "a_ready", a_m(p, g, 8))
            if not first:
                act_pt(act, p, g - 1)
            for pr in range(2):
                act.wait_ge(s["nmx"], (g * 2) + (2 * GROUPS * p + pr + 1))
                for q in range(4):
                    e = act.activation(pw[:, pr, q * P:(q + 1) * P], c_bank(pr)[:, q * P:(q + 1) * P], ACT.Exp,
                                       bias=nmx[:, pr, q:q + 1], scale=SCALE_A, accum_out=rs[:, pr, q:q + 1])
                e.then_inc(s["c_free"], 1)
            act_split_a(act, p, g + 1, "c_ready", c_s(p, g, 2))

        def act_pt(act, p, g):
            for pr in range(2):
                act.wait_ge(s["c_ready"], c_t(p, g, pr) + 1)
                dst = ptf[:, g, pr, :] if isinstance(g, int) else ptf[:, bass.ds(g, 1), pr, :]
                src = c_bank(pr)[:] if isinstance(g, int) else c_bank(pr)[:].rearrange("p (a n) -> p a n", a=1)
                act.activation(dst, src, ACT.Copy).then_inc(s["c_free"], 1)

        def act_values(act, p, g, last):
            k = g + GROUPS
            act.wait_ge(s["c_ready"], c_out(p, g, 0))
            act.wait_ge(s["c_free"], C_TILES * p + 4 * GROUPS)
            src = ptf[:, g] if isinstance(g, int) else ptf[:, bass.ds(g, 1)].rearrange("p a b n -> p (a b) n")
            act.activation(pth[:], src, ACT.Copy).then_inc(s["pth"], 1)

            def v_high(i):
                for j in range(TJ):
                    u = TJ * i + j
                    act.wait_ge(s["tmp"], mv_v(p, g, u + 1))
                    act.activation(vh[:, j, :], tmp[:, u % 2, :], ACT.Copy).then_inc(s["mvh"], 1)

            def z_high(i):
                for h in range(HG):
                    u = HG * i + h
                    act.wait_ge(s["b_ready"], b_z(p, g, u + 1))
                    act.activation(zh[:, h, :], b_bank(u)[:], ACT.Copy).then_inc(s["gzh"], 1)

            v_high(0)
            z_high(0)
            v_high(1)
            if not last:
                act_split_a(act, *nxt(p, k), "a_ready", a_v(p, g, 8))
            z_high(1)
            if not last:
                act_split_b(act, *nxt(p, k), "b_ready", b_z(p, g, 8))
            if p == 0:
                act.wait_ge(s["w_raw"], g * 48 + 48)
                for w in range(3):
                    part = wsum[0:WP, w, bass.ds(g, 1)]
                    act.activation(wraw[:, w, :], wraw[:, w, :], ACT.Abs, accum_out=part).then_inc(s["w_abs"], 1)

        def nxt(p, k):
            if isinstance(k, int) and k == W_LOADS - 1:
                return p + 1, 0
            return p, k + 1

        @block.scalar
        def _(act):
            credit(act, "act")
            for p in range(PASSES):
                act_norm(act, p)
                if p == 0:
                    act.wait_ge(s["w_pad"], 1)
                    act_split_b(act, 0, 0, None, 0)
                    act_split_a(act, 0, 0, None, 0)
                act_scores(act, p, 0, True)
                with act.Fori(1, GROUPS) as g:
                    act_scores(act, p, g, False)
                act_pt(act, p, GROUPS - 1)
                with act.Fori(0, GROUPS - 1) as g:
                    act_values(act, p, g, False)
                act_values(act, p, GROUPS - 1, p == PASSES - 1)
            stage_b_act(act)

        chain = [0]

        def make_link(dve, name, chain):
            def link(ins):
                chain[0] += 1
                ins.then_inc(s[name], 1)
                dve.wait_ge(s[name], chain[0])
            return link

        def dve_stats(dve, link, src):
            for j in range(TJ):
                link(dve.bn_stats(bst[:, j, :], src[:, j, :]))
            for j in range(TJ):
                link(dve.bn_aggr(mvar[:, j, :], bst[:, j, :]))
            link(dve.tensor_copy(nvar[:], mvar[:, :, 1]))
            newton_rsqrt(dve, link, rstd[:], ntmp[:], nvar[:])

        def dve_norm(dve, link, p):
            for i in range(PB):
                n = PB * TJ * p + TJ * i
                dve.wait_ge(s[f"x_in{i}"], 16 * (p + 1))
                dve_stats(dve, link, xacc[:, i])
                if n:
                    dve.wait_ge(s["a_ready"], a_xt(p, CK * i) if i else a_xt(p - 1, PB * CK))
                    dve.wait_ge(s["xl"], n)
                    dve.wait_ge(s["ph"], n)
                    dve.wait_ge(s["pl"], n)
                for j in range(TJ):
                    dve.tensor_scalar(xnf[:, j, :], xacc[:, i, j, :], mvar[:, j, 0:1], rstd[:, j:j + 1],
                                      ALU.subtract, ALU.mult).then_inc(s["xn"], 1)
                dve.wait_ge(s["xn"], n + TJ)
                for j in range(TJ):
                    dve.wait_ge(s["ph"], n + j + 1)
                    dve.scalar_tensor_tensor(pl[:, j, :], xnf[:, j, :], SHIFT, ph[:, j, :].bitcast(F32),
                                             ALU.add, ALU.subtract).then_inc(s["pl"], 1)
                for c in range(CK):
                    u = CK * i + c
                    dve.wait_ge(s["xth"], PB * CK * p + u + 1)
                    dve.tensor_tensor(xtl[:, i, c, :], a_bank(u)[:], xth[:, i, c, :].bitcast(F32),
                                      ALU.subtract).then_inc(s["xtl"], 1)
                    dve.reduce_sum(shat[:, i, c:c + 1], a_bank(u)[:], axis=AX).then_inc(s["a_free"], 1)
                for c in range(CK):
                    u = CK * i + c
                    dve.wait_ge(s["gzh"], b_g(p, u) + 1)
                    dve.tensor_tensor(gl[:, i, c, :], b_bank(u)[:], gh[:, i, c, :].bitcast(F32),
                                      ALU.subtract).then_inc(s["b_free"], 1)
            dve.wait_ge(s["a_free"], a_xt(p, PB * CK))
            dve.tensor_scalar(shat[:], shat[:], SHIFT * T, None, ALU.add).then_inc(s["shat"], 1)
            dve.wait_ge(s["shat"], p + 1)

        def dve_beta(dve, link):
            for g in range(GROUPS):
                dve.wait_ge(s["raw_a"], 16 * (g + 1))
                dve.reduce_sum(cs[:, HG * g:HG * (g + 1)], raw_a[:], axis=AX).then_inc(s["colsum"], 1)
            dve.wait_ge(s["colsum"], GROUPS)
            dve.wait_ge(s["bq_in"], 16)
            link(dve.scalar_tensor_tensor(betac[:], cs[:], -SHIFT, bqc[:], ALU.mult, ALU.add))
            dve.tensor_scalar(betac[:], betac[:], 1.0 / (C * SHIFT), None, ALU.mult).then_inc(s["beta_col"], 1)

        def dve_beta_add(dve, p, k):
            dve.wait_ge(s["raw_a"], load_of(p, k) * 32 + (16 * GROUPS + 32))
            for c in range(CK):
                dve.tensor_tensor(raw_a[:, c, :], raw_a[:, c, :], beta_bc[:], ALU.add).then_inc(s["beta_add"], 1)

        def dve_scores(dve, p, g):
            dve.wait_ge(s["bkv_in"], load_of(p, g) * 16 + 16)
            for u in range(8):
                i, c = u // CK, u % CK
                dve.wait_ge(s["a_ready"], a_m(p, g, u + 1))
                if not (p == 0 and isinstance(g, int) and u < 2):
                    dve.wait_ge(s["mvl"], mv_m(p, g, u - 1))
                dve.scalar_tensor_tensor(tmp[:, u % 2, :], bkv_bc[:], shat[:, i, c:c + 1], a_bank(u)[:],
                                         ALU.mult, ALU.add).then_inc(s["tmp"], 1)
                dve_release(dve, u, p, g, mv_m)
            for pr in range(2):
                n = (g * 2) + (2 * GROUPS * p + pr + 1)
                dve.wait_ge(s["c_ready"], c_s(p, g, pr) + 1)
                if p or not isinstance(g, int):
                    dve.wait_ge(s["c_free"], c_s(p, g, pr) - 3)
                dve.reduce_max(mx[:, pr, :], c_bank(pr)[:].rearrange("p (a n) -> p a n", n=P), axis=AX).then_inc(s["mx"], 1)
                dve.wait_ge(s["mx"], n)
                dve.tensor_scalar(nmx[:, pr, :], mx[:, pr, :], -SCALE_A, None, ALU.mult).then_inc(s["nmx"], 1)
            for pr in range(2):
                n = (g * 2) + (2 * GROUPS * p + pr + 1)
                dve.wait_ge(s["c_free"], c_s(p, g, pr) + 1)
                dve.reciprocal(rinv[:, pr, :], rs[:, pr, :]).then_inc(s["rinv"], 1)
                dve.wait_ge(s["rinv"], n)
                w = pw[:, pr, :].rearrange("p (a n) -> p a n", n=P)
                dve.tensor_tensor(w, w, rinv[:, pr, :].rearrange("p (a n) -> p a n", n=1).to_broadcast([P, 4, P]),
                                  ALU.mult).then_inc(s["pn"], 1)
            dve_beta_add(dve, p, g + 1)

        def dve_release(dve, u, p, g, mv):
            dve.wait_ge(s["tmp"], mv(p, g, u + 1))
            dve.sem_inc(s["a_free"], 1)

        def dve_values(dve, p, g, last):
            k = g + GROUPS
            dve.wait_ge(s["bkv_in"], load_of(p, k) * 16 + 16)

            def v_bias(i):
                for j in range(TJ):
                    u = TJ * i + j
                    dve.wait_ge(s["a_ready"], a_v(p, g, u + 1))
                    dve.wait_ge(s["mvl"], mv_v(p, g, u - 1))
                    dve.tensor_tensor(tmp[:, u % 2, :], a_bank(u)[:], bkv_bc[:], ALU.add).then_inc(s["tmp"], 1)
                    dve_release(dve, u, p, g, mv_v)

            def z_low(i):
                for h in range(HG):
                    u = HG * i + h
                    dve.wait_ge(s["gzh"], b_z(p, g, u + 1))
                    dve.tensor_tensor(zl[:, h, :], b_bank(u)[:], zh[:, h, :].bitcast(F32),
                                      ALU.subtract).then_inc(s["b_free"], 1)

            def add_out(i):
                if i == 0:
                    dve.wait_ge(s["xacc_bo"], PB * TJ * (p + 1))
                for h in range(HG):
                    u = HG * i + h
                    dve.wait_ge(s["c_ready"], c_out(p, g, u + 1))
                    dve.tensor_tensor(xacc[:, i, h, :], xacc[:, i, h, :], c_bank(u)[:], ALU.add).then_inc(s["c_free"], 1)

            v_bias(0)
            z_low(0)
            v_bias(1)
            add_out(0)
            if not last:
                dve_beta_add(dve, *nxt(p, k))
            z_low(1)
            add_out(1)
            if p == 1:
                dve_ternary(dve, g)

        def dve_weight_sums(dve):
            dve.wait_ge(s["w_abs"], 1 + 3 * GROUPS)
            dve.reduce_sum(wmean[:], wsum[:], axis=AX).then_inc(s["w_sum"], 1)

        def dve_weight_means(dve, link):
            dve.wait_ge(s["w_sum"], 2)
            link(dve.tensor_scalar(wmean[:], wthr[:, 0, :], 1.0 / (HID * C), None, ALU.mult))
            link(dve.tensor_scalar(wthr[:, 0, :], wmean[:], 0.5, None, ALU.mult))
            link(dve.tensor_scalar(wthr[:, 1, :], wmean[:], -0.5, None, ALU.mult))
            link(dve.tensor_tensor(wscale[:], wthr[:, 0, 0:1], wmean[:, 1:2], ALU.mult))

        def dve_ternary(dve, g):
            dve.wait_ge(s["w_raw"], g * 48 + (48 * GROUPS + 48))
            for w in range(3):
                dve.wait_ge(s["w_q"], 1 + g * 3 + w)
                dve.tensor_scalar(wlow[:], wraw[:, w, :], wthr[0:WP, 1, w:w + 1], None, ALU.is_lt).then_inc(s["w_low"], 1)
                dve.wait_ge(s["w_low"], g * 3 + (w + 1))
                dve.scalar_tensor_tensor(wraw[:, w, :], wraw[:, w, :], wthr[0:WP, 0, w:w + 1], wlow[:],
                                         ALU.is_gt, ALU.subtract).then_inc(s["w_q"], 1)

        def dve_x1(dve, link, p):
            for i in range(PB):
                dve.wait_ge(s["c_free"], c_out(p, GROUPS - 1, HG * (i + 1)))
                dve_stats(dve, link, xacc[:, i])
                link(dve.tensor_copy(stat[:, i, :, 0], mvar[:, :, 0]))
                dve.tensor_scalar(stat[:, i, :, 1], rstd[:], SCALE_X, None, ALU.mult).then_inc(s["x1_ready"], 1)
                dve.wait_ge(s["x1_ready"], PB * p + i + 1)

        @block.vector
        def _(dve):
            credit(dve, "dve")
            link = make_link(dve, "link", chain)
            for p in range(PASSES):
                if p == 1:
                    dve_weight_sums(dve)
                dve_norm(dve, link, p)
                if p == 1:
                    dve_weight_means(dve, link)
                if p == 0:
                    dve.memset(pw[0:1, 0, :], 0.0).then_inc(s["zero_beta"], 1)
                    dve_beta(dve, link)
                    dve_beta_add(dve, 0, 0)
                dve_scores(dve, p, 0)
                with dve.Fori(1, GROUPS) as g:
                    dve_scores(dve, p, g)
                with dve.Fori(0, GROUPS - 1) as g:
                    dve_values(dve, p, g, False)
                dve_values(dve, p, GROUPS - 1, p == PASSES - 1)
                dve_x1(dve, link, p)
            stage_b_dve(dve)

        def pool_norm(pool, p):
            for i in range(PB):
                n = PB * TJ * p + TJ * i
                for j in range(TJ):
                    pool.wait_ge(s["xh"], n + j + 1)
                    pool.tensor_tensor(xl[:, j, :], xnf[:, j, :], xh[:, j, :].bitcast(F32), ALU.subtract).then_inc(s["xl"], 1)
                if n == 0:
                    pool.wait_ge(s["bo_in"], 16)
                for j in range(TJ):
                    pool.wait_ge(s["xn"], n + TJ)
                    pool.tensor_tensor(xacc[:, i, j, :], xacc[:, i, j, :], bo_bc[:], ALU.add).then_inc(s["xacc_bo"], 1)

        def pool_split(pool, which, p, k):
            high, low, raw = {"a": (wah, wal, raw_a), "b": (wbh, wbl, raw_b)}[which]
            for c in range(CK):
                pool.wait_ge(s[f"w{which}h"], load_of(p, k) * CK + (c + 1))
                pool.tensor_tensor(low[:, c, :], raw[:, c, :], high[:, c, :].bitcast(F32),
                                   ALU.subtract).then_inc(s[f"w{which}l"], 1)

        def pool_low(pool, dst, slot, index):
            pool.wait_ge(s["mvh"], index + 1)
            high, low = dst
            pool.tensor_tensor(low, tmp[:, slot, :], high.bitcast(F32), ALU.subtract).then_inc(s["mvl"], 1)

        def pool_scores(pool, p, g):
            for u in range(8):
                i, c = u // CK, u % CK
                pool_low(pool, (mh[:, c, i, :], ml[:, c, i, :]), u % 2, mv_m(p, g, u))
            pool_split(pool, "b", p, g + 1)
            pool_split(pool, "a", p, g + 1)

        def pool_values(pool, p, g, last):
            k = g + GROUPS
            pool.wait_ge(s["pth"], g + (GROUPS * p + 1))
            src = ptf[:, g] if isinstance(g, int) else ptf[:, bass.ds(g, 1)].rearrange("p a b n -> p (a b) n")
            pool.tensor_tensor(ptl[:], src, pth[:].bitcast(F32), ALU.subtract).then_inc(s["ptl"], 1)
            for u in range(8):
                pool_low(pool, (vh[:, u % TJ, :], vl[:, u % TJ, :]), u % 2, mv_v(p, g, u))
            if not last:
                pool_split(pool, "a", *nxt(p, k))
                pool_split(pool, "b", *nxt(p, k))

        @block.gpsimd
        def _(pool):
            credit(pool, "pool")
            pool.memset(ident[:], 0.0).then_inc(s["ident"], 1)
            pool.wait_ge(s["ident"], 1)
            pool.affine_select(out=ident[:], in_=ident[:], compare_op=ALU.not_equal, fill=1.0, base=0,
                               pattern=[[-1, P]], channel_multiplier=1).then_inc(s["ident"], 1)
            pool.memset(wsum[:], 0.0).then_inc(s["w_pad"], 1)
            for p in range(PASSES):
                if p == 1:
                    pool.wait_ge(s["w_sum"], 1)
                    pool.partition_all_reduce(wthr[:, 0, :], wmean[:], P, bass.bass_isa.ReduceOp.add).then_inc(s["w_sum"], 1)
                pool_norm(pool, p)
                if p == 0:
                    pool_split(pool, "b", 0, 0)
                    pool_split(pool, "a", 0, 0)
                pool_scores(pool, p, 0)
                with pool.Fori(1, GROUPS) as g:
                    pool_scores(pool, p, g)
                with pool.Fori(0, GROUPS - 1) as g:
                    pool_values(pool, p, g, False)
                pool_values(pool, p, GROUPS - 1, p == PASSES - 1)
            stage_b_pool(pool)


def kernel(x, ctx_2048, L0_attn_Wq, L0_attn_bq, L0_attn_Wk, L0_attn_bk, L0_attn_Wv, L0_attn_bv, L0_attn_Wo, L0_attn_bo,
           L0_xattn_gamma, L0_ffn_w1, L0_ffn_w3, L0_ffn_w2):
    import numpy as np
    import concourse.bacc as bacc
    from concourse.bass_utils import run_bass_kernel_spmd

    D = np.asarray(L0_attn_Wq).shape[0]

    def by_group(w):
        return np.asarray(w).reshape(D, P, NH // GROUPS, GROUPS).transpose(3, 0, 2, 1).reshape(GROUPS, D, HG * P)

    def bias_by_group(b):
        return np.asarray(b).reshape(P, NH // GROUPS, GROUPS).transpose(2, 1, 0).reshape(GROUPS, HG * P)

    wq, wk, wv = by_group(L0_attn_Wq), by_group(L0_attn_Wk), by_group(L0_attn_Wv)
    wo = np.asarray(L0_attn_Wo).reshape(GROUPS, P, TJ, D).transpose(0, 2, 1, 3).reshape(GROUPS, T, D)
    arrays = {
        "x": x, "ctx": ctx_2048,
        "wa": np.concatenate([wq, wv]), "wb": np.concatenate([wk, wo]),
        "wq_t": wq.reshape(GROUPS, D, HG, P).transpose(0, 3, 2, 1),
        "bq_col": np.asarray(L0_attn_bq).reshape(P, HG, GROUPS).transpose(0, 2, 1).reshape(P, NH),
        "bkv": np.concatenate([bias_by_group(L0_attn_bk), bias_by_group(L0_attn_bv)]),
        "bo": L0_attn_bo, "gamma": np.asarray(L0_xattn_gamma).reshape(1, 1),
        "w1t": np.asarray(L0_ffn_w1).T, "w3t": np.asarray(L0_ffn_w3).T, "w2t": np.asarray(L0_ffn_w2).T,
    }
    arrays = {k: np.ascontiguousarray(v) for k, v in arrays.items()}
    nc = bacc.Bacc("TRN2", target_bir_lowering=False, num_devices=1)
    args = [nc.dram_tensor("in_" + k, v.shape, mybir.dt.from_np(v.dtype), kind="ExternalInput").ap() for k, v in arrays.items()]
    out = nc.dram_tensor("out_0", (B, T, C), F32, kind="ExternalOutput").ap()
    decoder_block(nc, *args, out)
    r = run_bass_kernel_spmd(nc, [{"in_" + k: v for k, v in arrays.items()}], core_ids=[0])
    return r.results[0]["out_0"]
```

```python
from contextlib import ExitStack

import concourse.bass as bass
from concourse import mybir

F32 = mybir.dt.float32
F32R = mybir.dt.float32r
I32 = mybir.dt.int32
ACT = mybir.ActivationFunctionType
ALU = mybir.AluOpType
AX = mybir.AxisListType.X

P = 128
B, T, C = 4, 512, 512
CK = C // P
TJ = T // P
NH, HG = 16, 4
GROUPS = NH // HG
PB = 2
PASSES = B // PB
EPS = 1e-5
SCALE_A = float(P) ** -0.5
XH, XD = 8, 64
SCALE_X = float(XD) ** -0.5
HID = int(2 * C * 4 / 3)
HC = -(-HID // P)
HP = HC * P
SHIFT = 0.125

WP = 105
WS = HID * C // WP // GROUPS
assert WP * WS * GROUPS == HID * C
RING_A, RING_B, RING_C = 4, 2, 2
A_TILES = PB * CK + 2 * GROUPS * PB * CK
B_TILES = PB * CK + GROUPS * PB * CK
C_TILES = 4 * GROUPS + GROUPS * PB * HG
MV = 2 * GROUPS * PB * CK
W_LOADS = 2 * GROUPS
Z1_EARLY = 2
FIRST_SPLIT = 3
TERNARY_AT = 1
T_AFTER = 4
TANH_LAG, GATE_LAG = 1, 1


def newton_rsqrt(dve, link, y, tmp, v):
    link(dve.tensor_scalar(v, v, EPS, None, ALU.add))
    link(dve.tensor_scalar(tmp.bitcast(I32), v.bitcast(I32), 1, None, ALU.logical_shift_right))
    link(dve.tensor_scalar(y.bitcast(I32), tmp.bitcast(I32), -1.0, float(0x5F3759DF), ALU.mult, ALU.add))
    for _ in range(3):
        link(dve.tensor_tensor(tmp, y, y, ALU.mult))
        link(dve.scalar_tensor_tensor(tmp, tmp, -0.5, v, ALU.mult, ALU.mult))
        link(dve.scalar_tensor_tensor(y, tmp, 1.5, y, ALU.add, ALU.mult))


def three_passes(pe, out, wh, wl, xh, xl, start, stop):
    pe.matmul(out, wh, xh, start=start, stop=False)
    pe.matmul(out, wh, xl, start=False, stop=False)
    return pe.matmul(out, wl, xh, start=False, stop=stop)


def decoder_block(nc, x, ctx, wa, wb, wq_t, bq_col, bkv, bo, gamma, w1t, w3t, w2t, out):
    x1_dram = nc.dram_tensor("x1_scratch", [B, T, C], F32, kind="Internal").ap()
    stat_dram = nc.dram_tensor("stat_scratch", [B, T, 2], F32, kind="Internal").ap()
    beta_dram = nc.dram_tensor("beta_scratch", [W_LOADS, HG * P], F32, kind="Internal").ap()
    wq_dram = [nc.dram_tensor(f"ternary_scratch{w}", list(v.shape), F32, kind="Internal").ap()
               for w, v in enumerate((w1t, w3t, w2t))]
    w_flat = [v.rearrange("a b -> (a b)").rearrange("(p n) -> p n", p=WP) for v in (w1t, w3t, w2t)]
    wq_flat = [v.rearrange("a b -> (a b)").rearrange("(p n) -> p n", p=WP) for v in wq_dram]
    stack = ExitStack()
    with stack:
        def sem(name):
            return stack.enter_context(nc.semaphore(name))

        s = {}
        for name in (
            "ident", "x_in0", "x_in1", "xn_in", "wqt_in", "bo_in", "bq_in", "raw_a", "raw_b", "bkv_in", "colsum", "beta_col", "beta_out", "link",
            "xn", "xh", "ph", "xl", "pl", "xacc_bo", "xth", "xtl", "shat", "gzh",
            "a_ready", "a_free", "b_ready", "b_free", "c_ready", "c_free",
            "wah", "wal", "wbh", "wbl", "beta_add", "tmp", "mvh", "mvl",
            "mx", "nmx", "rinv", "pn", "pth", "ptl", "x1_ready", "x1_out", "zero_beta",
            "const_in", "w_raw", "w_abs", "w_sum", "w_thr", "w_q", "w_scale", "w_pad", "w_low", "w_stored", "gam",
            "x1d_in0", "x1d_in1", "kd_in0", "kd_in1", "gam_in", "w_in", "x2_in", "x2_kept", "r_half", "u0_ready", "u1_ready", "u0_free", "u1_free", "gh2", "gl2", "y_ready", "st_in", "xq", "qh", "ql", "kh", "kl", "vth", "vtl", "x2",
            "s_ready", "s_free", "t_ready", "t_free", "r_ready", "r_free", "f_ready", "f_free",
            "xmx", "xnmx", "xrinv", "xpn", "pxh", "pxl", "r_sum", "x3n", "x3h", "x3l", "link_b",
            "tanh", "gate_sp", "gate_dve", "gate_pool", "u", "g", "gh", "gl", "y", "y_out",
        ):
            s[name] = sem("s_" + name)
        ident = stack.enter_context(nc.sbuf_tensor("ident", [P, P], F32))
        wsum = stack.enter_context(nc.sbuf_tensor("wsum", [P, 3, GROUPS], F32))
        wmean = stack.enter_context(nc.sbuf_tensor("wmean", [P, 3], F32))
        wthr = stack.enter_context(nc.sbuf_tensor("wthr", [P, 2, 3], F32))
        wscale = stack.enter_context(nc.sbuf_tensor("wscale", [P, 1], F32))
        bank = [stack.enter_context(nc.psum_tensor(f"bank{i}", [P, 512], F32)) for i in range(8)]

        CREDIT = {"dve": ("y", "u0_free", "u1_free", "w_q"), "act": ("w_abs",), "pool": ("gl2",), "sp": ("w_stored", "y_out")}

        def credit(eng, name):
            for c in CREDIT[name]:
                eng.sem_inc(s[c], 1)

        def gate(eng, name):
            eng.sem_inc(s["gate_" + name], 1)

        mem_a = ExitStack()

        def sa(name, shape, dt=F32):
            return mem_a.enter_context(nc.sbuf_tensor(name, shape, dt))

        work = sa("work", [P, 16, 512], F32R)
        xh, xl, ph, pl = (work[:, 4 * i:4 * i + 4, :] for i in range(4))
        mh = work[:, 0:8, :].rearrange("p (k b) n -> p k b n", b=PB)
        ml = work[:, 8:16, :].rearrange("p (k b) n -> p k b n", b=PB)
        vh, vl, zh, zl = xh, xl, ph, pl
        wbh, wbl = sa("wbh", [P, CK, 512], F32R), sa("wbl", [P, CK, 512], F32R)
        tmp = sa("tmp", [P, 2, 512])
        pth, ptl = sa("pth", [P, 2, 512], F32R), sa("ptl", [P, 2, 512], F32R)
        xacc = sa("xacc", [P, PB, TJ, C])
        bkv_bc = sa("bkv_bc", [P, 512])
        bst = sa("bst", [P, TJ, 6])
        mvar = sa("mvar", [P, TJ, 2])
        rstd, ntmp, nvar = sa("rstd", [P, TJ]), sa("ntmp", [P, TJ]), sa("nvar", [P, TJ])
        stat = sa("stat", [P, PB, TJ, 2])
        bqc, cs, betac = sa("bqc", [P, NH]), sa("cs", [P, NH]), sa("betac", [P, NH])
        shat = sa("shat", [P, PB, CK])
        mx, nmx = sa("mx", [P, 2, 4]), sa("nmx", [P, 2, 4])
        rs, rinv = sa("rs", [P, 2, 4]), sa("rinv", [P, 2, 4])
        mem_w = ExitStack()
        wraw = mem_w.enter_context(nc.sbuf_tensor("wraw", [WP, 3, WS], F32))
        wlow = mem_w.enter_context(nc.sbuf_tensor("wlow", [WP, WS], F32))
        mem_w.close()
        gh, gl = sa("gh", [P, PB, CK, C], F32R), sa("gl", [P, PB, CK, C], F32R)
        xth, xtl = sa("xth", [P, PB, CK, T], F32R), sa("xtl", [P, PB, CK, T], F32R)
        mem_q = ExitStack()
        wqt = [mem_q.enter_context(nc.sbuf_tensor(f"wqt{g}", [P, HG, 512], F32)) for g in range(2)]
        mem_q.close()
        wah, wal = sa("wah", [P, CK, 512], F32R), sa("wal", [P, CK, 512], F32R)
        raw_a, raw_b = sa("raw_a", [P, CK, 512]), sa("raw_b", [P, CK, 512])
        beta_bc, bo_bc = sa("beta_bc", [P, 512]), sa("bo_bc", [P, C])
        xnf0 = sa("xnf0", [P, TJ, C])
        ptf = sa("ptf", [P, GROUPS, 2, 512])
        xnf = [xnf0, ptf[:, 0:2].rearrange("p a b n -> p (a b) n")]
        wqt += [raw_a, ptf[:, 2:4].rearrange("p a b n -> p (a b) n")]
        pw = sa("pw", [P, 2, 512])
        mem_a.close()

        def a_bank(u):
            return bank[u % RING_A]

        def b_bank(u):
            return bank[RING_A + u % RING_B]

        def c_bank(u):
            return bank[RING_A + RING_B + u % RING_C]

        def a_xt(p, u):
            return A_TILES * p + u

        def a_m(p, g, u):
            return g * 8 + (A_TILES * p + PB * CK + u)

        def a_v(p, g, u):
            return g * 8 + (A_TILES * p + PB * CK + GROUPS * 8 + u)

        def b_g(p, u):
            return B_TILES * p + u

        def b_z(p, g, u):
            return g * 8 + (B_TILES * p + PB * CK + u)

        def c_s(p, g, pr):
            return g * 4 + (C_TILES * p + pr)

        def c_t(p, g, pr):
            return g * 4 + (C_TILES * p + 2 + pr)

        def c_out(p, g, u):
            return g * 8 + (C_TILES * p + 4 * GROUPS + u)

        def mv_m(p, g, u):
            return g * 8 + (MV * p + u)

        def mv_v(p, g, u):
            return g * 8 + (MV * p + GROUPS * 8 + u)

        def load_of(p, k):
            return k + W_LOADS * p

        def wait_bank(eng, free, index, ring):
            if isinstance(index, int) and index < ring:
                return
            eng.wait_ge(s[free], index - (ring - 1))

        def last_step(p, k):
            return p == PASSES - 1 and isinstance(k, int) and k == W_LOADS - 1


        mem_b = ExitStack()

        def sb(name, shape, dt=F32):
            return mem_b.enter_context(nc.sbuf_tensor(name, shape, dt))

        w13 = sb("w13", [P, 2, CK, HID], F32R)
        w2 = sb("w2", [P, HC, C], F32R)
        gth, gtl = sb("gth", [P, HC, T], F32R), sb("gtl", [P, HC, T], F32R)
        x2res = sb("x2res", [P, TJ, C])
        th, uu, gf = sb("th", [P, T]), sb("uu", [P, T]), sb("gf", [P, T])
        x3h, x3l = sb("x3h", [P, CK, T], F32R), sb("x3l", [P, CK, T], F32R)
        pxh, pxl = sb("pxh", [P, CK, C], F32R), sb("pxl", [P, CK, C], F32R)
        x1d = sb("x1d", [P, 2, C])
        kd = sb("kd", [P, 2, C])
        qst = sb("qst", [P, 2, C], F32R)
        kh, kl = sb("kh", [P, 2, C], F32R), sb("kl", [P, 2, C], F32R)
        vts = sb("vts", [P, 4, CK, P], F32R)
        pe_x = sb("pe_x", [P, 4, C])
        x2 = sb("x2", [P, TJ, C])
        stx = sb("stx", [P, XH, 2])
        xmx, xrs, xri = sb("xmx", [P, 4]), sb("xrs", [P, 4]), sb("xri", [P, 4])
        gam = sb("gam", [P, 1])
        bst_b, mv_b = sb("bst_b", [P, TJ, 6]), sb("mv_b", [P, TJ, 2])
        rstd_b, ntmp_b, nvar_b = sb("rstd_b", [P, TJ]), sb("ntmp_b", [P, TJ]), sb("nvar_b", [P, TJ])
        mem_b.close()
        s_bank, t_bank, r_bank, u_bank = bank[0:2], bank[2:4], bank[4], bank[5:7]
        y_bank = [bank[7], bank[5]]

        S_TILES = 4 * XH
        T_TILES = XH + 4 * XH + TJ
        U_PIECES = 2 * HC
        LINK_B = 2 + 1 + 12

        def t_v(b, h):
            return b * T_TILES + (5 * h - 4 if h else 0)

        def t_p(b, h, q):
            return b * T_TILES + (5 * (h + 1) - 3 + q if h < XH - 1 else 5 * XH - 4 + q)

        def t_x3(b, t):
            return b * T_TILES + (XH + 4 * XH + t)

        def pieces(n):
            if n < 0 or n >= S_TILES:
                return range(0)
            return range(U_PIECES * n // S_TILES, U_PIECES * (n + 1) // S_TILES)

        def chunk_rows(i):
            return min(P, HID - P * i)

        def turns(engine_loop, body):
            body(0, None, 1)
            with engine_loop(1, B - 1) as b:
                body(b, b - 1, b + 1)
            body(B - 1, B - 2, None)
            body(None, B - 1, None)

        def rows(t, b):
            return t[b] if isinstance(b, int) else t[bass.ds(b, 1)].rearrange("a t c -> (a t) c")

        def sp_head(sp, b, h):
            slot, n = h % 2, b * XH + h
            if h >= 2 or not isinstance(b, int) or b > 0:
                sp.wait_ge(s["ql"], n - 1)
                gate(sp, "sp")
                sp.wait_ge(s["t_ready"], t_v(b, h - 2) + 1 if h >= 2 else t_v(b - 1, XH - 2 + h) + 1)
            for half in range(2):
                part = slice(XD * half, XD * (half + 1))
                sp.dma_start(x1d[part, slot, :], rows(x1_dram, b)[XD * h:XD * (h + 1), :]).then_inc(s[f"x1d_in{slot}"], 16)
                sp.dma_start(kd[part, slot, :], rows(ctx, b)[XD * h:XD * (h + 1), :]).then_inc(s[f"kd_in{slot}"], 16)

        def sp_stats(sp, b):
            if not isinstance(b, int) or b > 0:
                sp.wait_ge(s["xq"], b * XH)
            for half in range(2):
                sp.dma_start(stx[XD * half:XD * (half + 1)], rows(stat_dram, b).rearrange("(h p) c -> p h c", p=XD)).then_inc(s["st_in"], 16)

        def sp_rows(sp, b, f):
            if b is not None:
                sp_stats(sp, b)
                sp_head(sp, b, 0)
                sp_head(sp, b, 1)
            if f is not None:
                for t in range(TJ):
                    sp.wait_ge(s["y"], 1 + f * TJ + (t + 1))
                    sp.dma_start(rows(out, f)[t * P:(t + 1) * P, :], x2res[:, t, :]).then_inc(s["y_out"], 16)
            if b is not None:
                sp_head(sp, b, 2)
                sp.wait_ge(s["x2_kept"], b * TJ)
                sp.dma_start(x2[:], rows(x1_dram, b).rearrange("(t p) c -> p t c", p=P)).then_inc(s["x2_in"], 16)
                for h in range(3, XH):
                    sp_head(sp, b, h)

        def stage_b_sp(sp):
            sp.wait_ge(s["wal"], CK * W_LOADS * PASSES)
            sp.wait_ge(s["wbl"], CK * W_LOADS * PASSES)
            sp.wait_ge(s["ptl"], GROUPS * PASSES)
            sp.wait_ge(s["a_ready"], A_TILES * PASSES)
            sp.dma_start(gam[:], gamma.to_broadcast([P, 1])).then_inc(s["gam_in"], 16)
            sp_stats(sp, 0)
            sp_head(sp, 0, 0)
            sp_head(sp, 0, 1)
            sp_x1_store(sp, PASSES - 1, 0)
            sp_head(sp, 0, 2)
            sp.dma_start(x2[:], x1_dram[0].rearrange("(t p) c -> p t c", p=P)).then_inc(s["x2_in"], 16)
            sp_x1_store(sp, PASSES - 1, 1)
            for h in range(3, XH):
                sp_head(sp, 0, h)
            sp.wait_ge(s["x1_out"], 32 * B)
            sp.wait_ge(s["w_stored"], 1 + 48 * GROUPS)
            for w in range(2):
                sp.dma_start(w13[:, w].bitcast(F32), wq_dram[w].rearrange("(c p) n -> p c n", p=P)).then_inc(s["w_in"], 16)
            full = HC - 1
            sp.dma_start(w2[:, 0:full, :].bitcast(F32), wq_dram[2][0:full * P, :].rearrange("(c p) n -> p c n", p=P)).then_inc(s["w_in"], 16)
            sp.dma_start(w2[0:chunk_rows(full), full, :].bitcast(F32), wq_dram[2][full * P:HID, :]).then_inc(s["w_in"], 16)
            sp_rows(sp, 1, None)
            with sp.Fori(2, B) as b:
                sp_rows(sp, b, b - 2)
            sp_rows(sp, None, B - 2)
            sp_rows(sp, None, B - 1)
            sp.wait_ge(s["y_out"], 1 + 16 * TJ * B)
            sp.wait_ge(s["gate_dve"], B)
            sp.wait_ge(s["gate_pool"], B * S_TILES)
            sp.wait_ge(s["gate_sp"], 1)

        def pe_vt(pe, b, h):
            pe.wait_ge(s[f"kd_in{h % 2}"], b * 128 + 32 * (h // 2 + 1))
            pe_wait(pe, "t_free", t_v(b, h), 2)
            tb = t_bank[(5 * h - 4 if h else 0) % 2]
            for c in range(CK):
                mm = pe.transpose(tb[:, c * P:(c + 1) * P], kd[:, h % 2, c * P:(c + 1) * P], ident[:])
            mm.then_inc(s["t_ready"], 1)

        def pe_wait(pe, free, index, ring):
            if not isinstance(index, int) or index >= ring:
                pe.wait_ge(s[free], index - (ring - 1))

        def pe_pt(pe, b, h, q):
            pe.wait_ge(s["xpn"], b * S_TILES + (4 * h + q + 1))
            pe_wait(pe, "t_free", t_p(b, h, q), 2)
            tb = t_bank[t_p(0, h, q) % 2]
            for c in range(CK):
                mm = pe.transpose(tb[:, c * P:(c + 1) * P], pe_x[:, q, c * P:(c + 1) * P], ident[:])
            mm.then_inc(s["t_ready"], 1)

        def pe_sx(pe, b, h, q):
            if q == 0:
                pe.wait_ge(s["ql"], b * XH + (h + 1))
                pe.wait_ge(s["kl"], b * XH + (h + 1))
            pe_wait(pe, "s_free", b * S_TILES + (4 * h + q), 2)
            lhs = qst[:, h % 2, q * P:(q + 1) * P]
            pe.matmul(s_bank[q % 2][:], lhs, kh[:, h % 2, :], start=True, stop=False)
            pe.matmul(s_bank[q % 2][:], lhs, kl[:, h % 2, :], start=False, stop=True).then_inc(s["s_ready"], 1)

        def pe_ret(pe, b, h, half):
            n = b * XH + h
            pe.wait_ge(s["t_free"], t_p(b, h, 2 * half + 1) + 1)
            if half == 0:
                pe_wait(pe, "r_free", n, 1)
            cols = slice(2 * P * half, 2 * P * (half + 1))
            for c in range(CK):
                lhs = vts[:, h % 4, c, :]
                pe.matmul(r_bank[:, cols], lhs, pxh[:, c, cols], start=c == 0, stop=False)
                mm = pe.matmul(r_bank[:, cols], lhs, pxl[:, c, cols], start=False, stop=c == CK - 1)
            mm.then_inc(s["r_ready"], 1)

        def pe_up(pe, f, piece):
            i, w = piece // 2, piece % 2
            m = chunk_rows(i)
            if piece == 0:
                pe.wait_ge(s["w_in"], 64)
                pe.wait_ge(s["t_free"], t_x3(f, TJ))
                pe.wait_ge(s["y"], 1 + f * TJ)
            pe.wait_ge(s[f"u{w}_free"], 1 + f * HC + i)
            for c in range(CK):
                lhs = w13[:, w, c, i * P:i * P + m]
                pe.matmul(u_bank[w][0:m, :], lhs, x3h[:, c, :], start=c == 0, stop=False)
                mm = pe.matmul(u_bank[w][0:m, :], lhs, x3l[:, c, :], start=False, stop=c == CK - 1)
            mm.then_inc(s[f"u{w}_ready"], 1)

        def pe_down(pe, f, t):
            pe.wait_ge(s["gl2"], 1 + f * HC + HC)
            if t >= 2:
                pe.wait_ge(s["y"], 1 + f * TJ + (t - 1))
            if t == 1:
                pe.wait_ge(s["u0_free"], 1 + f * HC + HC)
            for i in range(HC):
                k = chunk_rows(i)
                pe.matmul(y_bank[t % 2][:], gth[0:k, i, t * P:(t + 1) * P], w2[0:k, i, :], start=i == 0, stop=False)
                mm = pe.matmul(y_bank[t % 2][:], gtl[0:k, i, t * P:(t + 1) * P], w2[0:k, i, :], start=False, stop=i == HC - 1)
            mm.then_inc(s["y_ready"], 1)

        def pe_x3(pe, b, t):
            pe.wait_ge(s["x3n"], b * TJ + (t + 1))
            pe_wait(pe, "t_free", t_x3(b, t), 2)
            tb = t_bank[t_x3(0, t) % 2]
            for c in range(CK):
                mm = pe.transpose(tb[:, c * P:(c + 1) * P], pe_x[:, t, c * P:(c + 1) * P], ident[:])
            mm.then_inc(s["t_ready"], 1)

        def pe_turn(pe, b, f, nxt):
            for h in range(XH):
                for q in range(4):
                    if b is not None:
                        pe_sx(pe, b, h, q)
                        if q == 0:
                            pe_vt(pe, b, h)
                        if h:
                            pe_pt(pe, b, h - 1, q)
                        if q == 1 and h >= 2:
                            pe_ret(pe, b, h - 2, 1)
                        if q == 3 and h >= 1:
                            pe_ret(pe, b, h - 1, 0)
                    if f is not None:
                        for piece in pieces(4 * h + q):
                            pe_up(pe, f, piece)
            if b is not None:
                pe_pt(pe, b, XH - 1, 0)
                pe_ret(pe, b, XH - 2, 1)
                pe_pt(pe, b, XH - 1, 1)
                pe_pt(pe, b, XH - 1, 2)
            if f is not None:
                pe_down(pe, f, 0)
            if b is not None:
                pe_pt(pe, b, XH - 1, 3)
                pe_ret(pe, b, XH - 1, 0)
                pe_ret(pe, b, XH - 1, 1)
            if f is not None:
                for t in range(1, TJ - 1):
                    pe_down(pe, f, t)
            if b is not None:
                pe_x3(pe, b, 0)
                pe_x3(pe, b, 1)
            if f is not None:
                pe_down(pe, f, TJ - 1)
            if b is not None:
                for t in range(2, TJ):
                    pe_x3(pe, b, t)

        def stage_b_pe(pe):
            turns(pe.Fori, lambda b, f, nxt: pe_turn(pe, b, f, nxt))

        def act_prep(act, b, h):
            n, slot = b * XH + h, h % 2
            act.wait_ge(s[f"kd_in{slot}"], b * 128 + 32 * (h // 2 + 1))
            if h >= 2 or not isinstance(b, int) or b > 0:
                act.wait_ge(s["s_ready"], b * S_TILES + 4 * (h - 1))
            act.activation(kh[:, slot, :], kd[:, slot, :], ACT.Copy).then_inc(s["kh"], 1)
            act.wait_ge(s["xq"], n + 1)
            act.activation(qst[:, slot, :], x1d[:, slot, :], ACT.Copy).then_inc(s["qh"], 1)

        def act_vt(act, b, h):
            tb = t_bank[(5 * h - 4 if h else 0) % 2][:].rearrange("p (c n) -> p c n", n=P)
            act.wait_ge(s["t_ready"], t_v(b, h) + 1)
            act.activation(vts[:, h % 4, :, 0:XD], tb[:, :, 0:XD], ACT.Copy).then_inc(s["vth"], 1)

        def act_px(act, b, h, q):
            tb = t_bank[t_p(0, h, q) % 2][:].rearrange("p (c n) -> p c n", n=P)
            act.wait_ge(s["t_ready"], t_p(b, h, q) + 1)
            act.activation(pxh[:, :, q * P:(q + 1) * P], tb, ACT.Copy).then_inc(s["pxh"], 1)

        def act_exp(act, b, h, q):
            act.wait_ge(s["xmx"], b * S_TILES + (4 * h + q + 1))
            act.activation(pe_x[:, q, :], s_bank[q % 2][:], ACT.Exp, bias=xmx[:, q:q + 1],
                           accum_out=xrs[:, q:q + 1]).then_inc(s["s_free"], 1)

        def act_tanh(act, f, piece):
            i, w = piece // 2, piece % 2
            m = chunk_rows(i)
            n = f * HC + i
            if w == 0:
                act.wait_ge(s["u0_ready"], n + 1)
                act.wait_ge(s["u0_free"], 1 + n)
                act.activation(th[0:m, :], u_bank[0][0:m, :], ACT.Tanh, scale=wthr[0:m, 0, 0:1]).then_inc(s["tanh"], 1)

        def act_gate(act, f, piece):
            i, w = piece // 2, piece % 2
            m = chunk_rows(i)
            if w:
                act.wait_ge(s["u1_free"], 1 + f * HC + i + 1)
                act.activation(gth[0:m, i, :], gf[0:m, :], ACT.Copy).then_inc(s["gh2"], 1)

        def act_keep(act, f, t):
            act.wait_ge(s["x3n"], (f + 1) * TJ)
            act.wait_ge(s["y_out"], 1 + f * (16 * TJ))
            act.activation(x2res[:, t, :], x2[:, t, :], ACT.Copy).then_inc(s["x2_kept"], 1)

        def act_turn(act, b, f, nxt):
            for n in range(S_TILES):
                h, q = n // 4, n % 4
                if f is not None:
                    for piece in pieces(n - TANH_LAG):
                        act_tanh(act, f, piece)
                if b is not None:
                    if q == 0:
                        act_vt(act, b, h)
                    if h:
                        act_px(act, b, h - 1, q)
                    act_exp(act, b, h, q)
                    if q == 0 and h + 1 < XH:
                        act_prep(act, b, h + 1)
                if f is not None:
                    if n < TJ:
                        act_keep(act, f, n)
                    for piece in pieces(n - GATE_LAG):
                        act_gate(act, f, piece)
            if f is not None:
                for n in range(S_TILES, S_TILES + GATE_LAG):
                    for piece in pieces(n - TANH_LAG):
                        act_tanh(act, f, piece)
                    for piece in pieces(n - GATE_LAG):
                        act_gate(act, f, piece)
            if b is not None:
                for q in range(4):
                    act_px(act, b, XH - 1, q)
                if nxt is not None:
                    act_prep(act, nxt, 0)
                for t in range(TJ):
                    tb = t_bank[t_x3(0, t) % 2][:].rearrange("p (c n) -> p c n", n=P)
                    act.wait_ge(s["t_ready"], t_x3(b, t) + 1)
                    act.activation(x3h[:, :, t * P:(t + 1) * P], tb, ACT.Copy).then_inc(s["x3h"], 1)

        def stage_b_act(act):
            turns(act.Fori, lambda b, f, nxt: act_turn(act, b, f, nxt))

        def dve_q(dve, b, h):
            n, slot = b * XH + h, h % 2
            dve.wait_ge(s[f"x1d_in{slot}"], b * 128 + 32 * (h // 2 + 1))
            if h == 0:
                dve.wait_ge(s["st_in"], b * 32 + 32)
            dve.tensor_scalar(x1d[:, slot, :], x1d[:, slot, :], stx[:, h, 0:1], stx[:, h, 1:2],
                              ALU.subtract, ALU.mult).then_inc(s["xq"], 1)

        def dve_vt(dve, b, h):
            tb = t_bank[(5 * h - 4 if h else 0) % 2][:].rearrange("p (c n) -> p c n", n=P)
            dve.wait_ge(s["vth"], b * XH + (h + 1))
            dve.tensor_tensor(vts[:, h % 4, :, XD:P], tb[:, :, XD:P], vts[:, h % 4, :, 0:XD].bitcast(F32),
                              ALU.subtract).then_inc(s["t_free"], 1)

        def dve_px(dve, b, h, q):
            tb = t_bank[t_p(0, h, q) % 2][:].rearrange("p (c n) -> p c n", n=P)
            dve.wait_ge(s["pxh"], b * S_TILES + (4 * h + q + 1))
            dve.tensor_tensor(pxl[:, :, q * P:(q + 1) * P], tb, pxh[:, :, q * P:(q + 1) * P].bitcast(F32),
                              ALU.subtract).then_inc(s["t_free"], 1)

        def dve_max(dve, b, h, q):
            dve.wait_ge(s["s_ready"], b * S_TILES + (4 * h + q + 1))
            dve.reduce_max(xmx[:, q:q + 1], s_bank[q % 2][:], axis=AX, negate=True).then_inc(s["xmx"], 1)

        def dve_rinv(dve, b, h, q):
            dve.wait_ge(s["s_free"], b * S_TILES + (4 * h + q + 1))
            dve.reciprocal(xri[:, q:q + 1], xrs[:, q:q + 1]).then_inc(s["xrinv"], 1)

        def dve_ret(dve, b, h):
            n = b * XH + h
            rows_ = slice(XD * (h % 2), XD * (h % 2) + XD)
            dve.wait_ge(s["r_ready"], 2 * n + 2)
            dst = x2[rows_, h // 2, :]
            if h == 0:
                dve.wait_ge(s["x2_in"], b * 16 + 16)
            dve.tensor_tensor(dst, dst, r_bank[0:XD, :], ALU.add).then_inc(s["r_half"], 1)
            dve.wait_ge(s["r_half"], n + 1)
            dve.tensor_tensor(dst, dst, r_bank[XD:P, :], ALU.add).then_inc(s["r_free"], 1)

        def dve_moments(dve, b, t):
            dve.wait_ge(s["r_free"], b * XH + 2 * (t + 1))
            dve.bn_stats(bst_b[:, t, :], x2[:, t, :])

        def dve_up(dve, f, piece):
            i, w = piece // 2, piece % 2
            m = chunk_rows(i)
            n = f * HC + i
            if w == 0:
                dve.wait_ge(s["tanh"], n + 1)
                dve.wait_ge(s["u1_free"], 1 + n)
                dve.scalar_tensor_tensor(uu[0:m, :], th[0:m, :], 1.0, u_bank[0][0:m, :], ALU.add, ALU.mult).then_inc(s["u0_free"], 1)
            else:
                dve.wait_ge(s["u1_ready"], n + 1)
                dve.wait_ge(s["u0_free"], 1 + n + 1)
                dve.wait_ge(s["gl2"], 1 + n)
                dve.scalar_tensor_tensor(gf[0:m, :], uu[0:m, :], wscale[0:m, 0:1], u_bank[1][0:m, :], ALU.mult, ALU.mult).then_inc(s["u1_free"], 1)

        def dve_y(dve, f, t):
            dve.wait_ge(s["y_ready"], f * TJ + (t + 1))
            if t == 0:
                dve.wait_ge(s["x2_kept"], f * TJ + TJ)
            dve.scalar_tensor_tensor(x2res[:, t, :], y_bank[t % 2][:], wmean[:, 2:3], x2res[:, t, :],
                                     ALU.mult, ALU.add).then_inc(s["y"], 1)

        def dve_x3(dve, b, count):
            def link(ins):
                count[0] += 1
                ins.then_inc(s["link_b"], 1)
                dve.wait_ge(s["link_b"], b * LINK_B + count[0])
            dve.wait_ge(s["r_free"], b * XH + XH)
            for t in range(TJ - 1, TJ):
                i = dve.bn_stats(bst_b[:, t, :], x2[:, t, :])
            link(i)
            gate(dve, "dve")
            for t in range(TJ):
                i = dve.bn_aggr(mv_b[:, t, :], bst_b[:, t, :])
            link(i)
            link(dve.tensor_copy(nvar_b[:], mv_b[:, :, 1]))
            newton_rsqrt(dve, link, rstd_b[:], ntmp_b[:], nvar_b[:])
            assert count[0] == LINK_B, count

        def dve_x3n(dve, b, t):
            dve.wait_ge(s["t_ready"], t_x3(b, 0))
            dve.tensor_scalar(pe_x[:, t, :], x2[:, t, :], mv_b[:, t, 0:1], rstd_b[:, t:t + 1], ALU.subtract, ALU.mult).then_inc(s["x3n"], 1)

        def dve_x3l(dve, b, t):
            tb = t_bank[t_x3(0, t) % 2][:].rearrange("p (c n) -> p c n", n=P)
            dve.wait_ge(s["x3h"], b * TJ + (t + 1))
            dve.tensor_tensor(x3l[:, :, t * P:(t + 1) * P], tb, x3h[:, :, t * P:(t + 1) * P].bitcast(F32),
                              ALU.subtract).then_inc(s["t_free"], 1)

        def dve_turn(dve, b, f, nxt, between=None):
            for n in range(S_TILES):
                h, q = n // 4, n % 4
                if b is not None:
                    if q == 2 and h >= 2:
                        dve_ret(dve, b, h - 2)
                    dve_max(dve, b, h, q)
                    if q == 0:
                        dve_vt(dve, b, h)
                if f is not None:
                    for piece in pieces(n - TANH_LAG):
                        dve_up(dve, f, piece)
                if b is not None:
                    if h:
                        dve_px(dve, b, h - 1, q)
                    if n:
                        dve_rinv(dve, b, (n - 1) // 4, (n - 1) % 4)
                    if q == 0 and h + 1 < XH:
                        dve_q(dve, b, h + 1)
                    if q == 0 and h >= 4 and h % 2 == 0:
                        dve_moments(dve, b, (h - 4) // 2)
                    if between:
                        between(n)
            if f is not None:
                for n in range(S_TILES, S_TILES + TANH_LAG):
                    for piece in pieces(n - TANH_LAG):
                        dve_up(dve, f, piece)
            if b is not None:
                dve_rinv(dve, b, XH - 1, 3)
                dve_px(dve, b, XH - 1, 0)
                dve_ret(dve, b, XH - 2)
                dve_px(dve, b, XH - 1, 1)
                dve_px(dve, b, XH - 1, 2)
                dve_moments(dve, b, TJ - 2)
                if nxt is not None:
                    dve_q(dve, nxt, 0)
            if f is not None:
                dve_y(dve, f, 0)
            if b is not None:
                dve_px(dve, b, XH - 1, 3)
                dve_ret(dve, b, XH - 1)
                dve_x3(dve, b, [0])
                for t in range(TJ):
                    dve_x3n(dve, b, t)
            if f is not None:
                for t in range(1, TJ - 1):
                    dve_y(dve, f, t)
            if b is not None:
                dve_x3l(dve, b, 0)
                dve_x3l(dve, b, 1)
            if f is not None:
                dve_y(dve, f, TJ - 1)
            if b is not None:
                for t in range(2, TJ):
                    dve_x3l(dve, b, t)

        def stage_b_dve(dve, link):
            def attention_rest(n):
                if n < 4:
                    dve_x1(dve, link, PASSES - 1, 1, n)
            turns(dve.Fori, lambda b, f, nxt: dve_turn(dve, b, f, nxt, attention_rest if f is None else None))

        def pool_prep(pool, b, h):
            n, slot = b * XH + h, h % 2
            pool.wait_ge(s["kh"], n + 1)
            pool.tensor_tensor(kl[:, slot, :], kd[:, slot, :], kh[:, slot, :].bitcast(F32), ALU.subtract).then_inc(s["kl"], 1)
            pool.wait_ge(s["qh"], n + 1)
            pool.wait_ge(s["kl"], n + 1)
            pool.tensor_tensor(qst[XD:P, slot, :], x1d[XD:P, slot, :], qst[XD:P, slot, :].bitcast(F32), ALU.subtract).then_inc(s["ql"], 1)
            pool.wait_ge(s["ql"], n + 1)

        def pool_prob(pool, b, h, q):
            pool.wait_ge(s["xrinv"], b * S_TILES + (4 * h + q + 1))
            gate(pool, "pool")
            pool.tensor_scalar(pe_x[:, q, :], pe_x[:, q, :], xri[:, q:q + 1], gam[:], ALU.mult, ALU.mult).then_inc(s["xpn"], 1)

        def pool_up(pool, f, piece):
            i, w = piece // 2, piece % 2
            if w:
                m = chunk_rows(i)
                pool.wait_ge(s["gh2"], f * HC + (i + 1))
                pool.tensor_tensor(gtl[0:m, i, :], gf[0:m, :], gth[0:m, i, :].bitcast(F32), ALU.subtract).then_inc(s["gl2"], 1)

        def pool_turn(pool, b, f, nxt):
            if isinstance(b, int) and b == 0:
                pool_prep(pool, b, 0)
            for n in range(S_TILES):
                h, q = n // 4, n % 4
                if b is not None:
                    if n:
                        pool_prob(pool, b, (n - 1) // 4, (n - 1) % 4)
                    if q == 0 and h + 1 < XH:
                        pool_prep(pool, b, h + 1)
                if f is not None:
                    for piece in pieces(n - GATE_LAG):
                        pool_up(pool, f, piece)
            if b is not None:
                pool_prob(pool, b, XH - 1, 3)
            if f is not None:
                for n in range(S_TILES, S_TILES + GATE_LAG):
                    for piece in pieces(n - GATE_LAG):
                        pool_up(pool, f, piece)
            if nxt is not None:
                pool_prep(pool, nxt, 0)

        def stage_b_pool(pool):
            pool.wait_ge(s["gam_in"], 16)
            turns(pool.Fori, lambda b, f, nxt: pool_turn(pool, b, f, nxt))

        def sp_raw_b(sp, p, k):
            sp.wait_ge(s["wbl"], CK * load_of(p, k))
            sp.dma_start(raw_b[:], wb[bass.ds(k, 1)].rearrange("a (c p) n -> (a p) c n", p=P)
                         if not isinstance(k, int) else wb[k].rearrange("(c p) n -> p c n", p=P)
                         ).then_inc(s["raw_b"], 16)

        def sp_raw_a(sp, p, k):
            sp.wait_ge(s["wal"], CK * load_of(p, k))
            if isinstance(k, int):
                src, brow = wa[k].rearrange("(c p) n -> p c n", p=P), beta_dram[k:k + 1, :]
            else:
                src = wa[bass.ds(k, 1)].rearrange("a (c p) n -> (a p) c n", p=P)
                brow = beta_dram[bass.ds(k, 1), :]
            sp.dma_start(raw_a[:], src).then_inc(s["raw_a"], 16)
            sp.dma_start(beta_bc[:], brow.to_broadcast([P, 512])).then_inc(s["raw_a"], 16)

        def sp_bkv(sp, p, k):
            sp.wait_ge(s["tmp"], 8 * load_of(p, k))
            row = bkv[k:k + 1, :] if isinstance(k, int) else bkv[bass.ds(k, 1), :]
            sp.dma_start(bkv_bc[:], row.to_broadcast([P, 512])).then_inc(s["bkv_in"], 16)

        def sp_step(sp, p, k):
            sp_raw_b(sp, p, k)
            sp_raw_a(sp, p, k)
            sp_bkv(sp, p, k)

        def sp_weights(sp, p, g):
            sp.wait_ge(s["a_ready"], a_m(p, GROUPS - 1, 8))
            if p == 0:
                sp.wait_ge(s["w_abs"], 1 + g * 3)
            else:
                sp.wait_ge(s["w_q"], 1 + g * 3)
                gate(sp, "sp")
                sp.wait_ge(s["w_stored"], 1 + g * 48)
            for w in range(3):
                sp.dma_start(wraw[:, w, :], w_flat[w][:, bass.ds(g * WS, WS)]).then_inc(s["w_raw"], 16)

        def sp_weights_out(sp, p, g):
            if p == 1:
                for w in range(3):
                    sp.wait_ge(s["w_q"], 1 + g * 3 + (w + 1))
                    sp.dma_start(wq_flat[w][:, bass.ds(g * WS, WS)], wraw[:, w, :]).then_inc(s["w_stored"], 16)

        def sp_x(sp, b):
            if b >= PB:
                sp.wait_ge(s["x1_out"], 32 * (b - PB + 1))
            sp.dma_start(xacc[:, b % PB], x[b].rearrange("(p j) c -> p j c", j=TJ)).then_inc(s[f"x_in{b % PB}"], 16)

        def sp_xn(sp, p, i):
            if p and i == 0:
                for name in ("xh", "ph", "xl", "pl"):
                    sp.wait_ge(s[name], PB * TJ * (p - 1) + TJ)
                sp.wait_ge(s["a_ready"], a_xt(p - 1, CK))
            elif p:
                sp.wait_ge(s["pth"], GROUPS * p)
                sp.wait_ge(s["ptl"], GROUPS * p)
            sp.dma_start(xnf[i][:], x[PB * p + i].rearrange("(p j) c -> p j c", j=TJ)).then_inc(s["xn_in"], 16)
            sp.wait_ge(s["xn_in"], 16 * (PB * p + i + 1))

        def sp_x1_store(sp, p, i):
            b = PB * p + i
            sp.wait_ge(s["x1_ready"], b + 1)
            sp.dma_start(x1_dram[b].rearrange("(p j) c -> p j c", j=TJ), xacc[:, i]).then_inc(s["x1_out"], 16)
            sp.dma_start(stat_dram[b].rearrange("(p j) c -> p j c", j=TJ), stat[:, i]).then_inc(s["x1_out"], 16)

        block = stack.enter_context(nc.Block())

        @block.sync
        def _(sp):
            credit(sp, "sp")
            sp_xn(sp, 0, 0)
            sp_raw_b(sp, 0, 0)
            for g in range(2):
                sp.dma_start(wqt[g][:], wq_t[g]).then_inc(s["wqt_in"], 16)
                sp.wait_ge(s["wqt_in"], 16 * (g + 1))
            sp_xn(sp, 0, 1)
            for g in range(2, GROUPS):
                sp.dma_start(wqt[g][:], wq_t[g]).then_inc(s["wqt_in"], 16)
                sp.wait_ge(s["wqt_in"], 16 * (g + 1))
            sp.dma_start(bqc[:], bq_col).then_inc(s["bq_in"], 16)
            sp.dma_start(bo_bc[:], bo.rearrange("(a n) -> a n", a=1).to_broadcast([P, C])).then_inc(s["bo_in"], 16)
            sp_x(sp, 0)
            sp_x(sp, 1)
            sp.wait_ge(s["beta_col"], 1)
            with nc.allow_non_contiguous_dma(reason="2048 words once"):
                sp.dma_start(beta_dram[0:GROUPS, :].rearrange("g (h n) -> n (g h)", n=P), betac[:]).then_inc(s["beta_out"], 16)
            sp.wait_ge(s["zero_beta"], 1)
            for g in range(GROUPS):
                sp.dma_start(beta_dram[GROUPS + g:GROUPS + g + 1, :], pw[0:1, 0, :]).then_inc(s["beta_out"], 16)
            sp.wait_ge(s["beta_out"], 16 * (GROUPS + 1))
            sp_raw_a(sp, 0, 0)
            sp_bkv(sp, 0, 0)
            for p in range(PASSES):
                with sp.Fori(2 if p else 1, GROUPS + 1) as k:
                    sp_step(sp, p, k)
                with sp.Fori(0, GROUPS - 1) as g:
                    sp_weights(sp, p, g)
                    sp_step(sp, p, g + GROUPS + 1)
                    sp_weights_out(sp, p, g)
                if p < PASSES - 1:
                    sp_xn(sp, p + 1, 0)
                    sp_xn(sp, p + 1, 1)
                sp_weights(sp, p, GROUPS - 1)
                sp_weights_out(sp, p, GROUPS - 1)
                if p < PASSES - 1:
                    sp_step_next = p + 1
                    sp_raw_b(sp, sp_step_next, 0)
                    sp_raw_a(sp, sp_step_next, 0)
                    sp_bkv(sp, sp_step_next, 0)
                    sp_raw_b(sp, p + 1, 1)
                    sp_raw_a(sp, p + 1, 1)
                    sp_x1_store(sp, p, 0)
                    sp_x(sp, PB * (p + 1))
                    sp_x1_store(sp, p, 1)
                    sp_bkv(sp, p + 1, 1)
                    sp_x(sp, PB * (p + 1) + 1)
            stage_b_sp(sp)

        def pe_norm(pe, p):
            for i in range(PB):
                n = PB * TJ * p + TJ * i
                pe.wait_ge(s["xn"], n + TJ)
                for c in range(CK):
                    u = CK * i + c
                    wait_bank(pe, "a_free", a_xt(p, u), RING_A)
                    for j in range(TJ):
                        mm = pe.transpose(a_bank(u)[:, j * P:(j + 1) * P], xnf[i][:, j, c * P:(c + 1) * P], ident[:])
                    mm.then_inc(s["a_ready"], 1)
                for c in range(CK):
                    u = CK * i + c
                    wait_bank(pe, "b_free", b_g(p, u), RING_B)
                    for j in range(TJ):
                        if c == 0:
                            pe.wait_ge(s["xl"], n + j + 1)
                            pe.wait_ge(s["pl"], n + j + 1)
                        mm = three_passes(pe, b_bank(u)[:], xh[:, j, c * P:(c + 1) * P], xl[:, j, c * P:(c + 1) * P],
                                          ph[:, j, :], pl[:, j, :], j == 0, j == TJ - 1)
                    mm.then_inc(s["b_ready"], 1)

        def pe_m(pe, p, g, between=None):
            for u in range(PB * CK):
                i, c = u // CK, u % CK
                if c == 0 and isinstance(g, int):
                    pe.wait_ge(s["gzh"], b_g(p, CK * (i + 1)))
                    pe.wait_ge(s["b_free"], b_g(p, CK * (i + 1)))
                wait_bank(pe, "a_free", a_m(p, g, u), RING_A)
                for k in range(CK):
                    if u == 0:
                        pe.wait_ge(s["wbl"], load_of(p, g) * CK + (k + 1))
                    mm = three_passes(pe, a_bank(u)[:], gh[:, i, k, c * P:(c + 1) * P], gl[:, i, k, c * P:(c + 1) * P],
                                      wbh[:, k, :], wbl[:, k, :], k == 0, k == CK - 1)
                mm.then_inc(s["a_ready"], 1)
                if between:
                    between(u)

        def pe_t(pe, p, g):
            for pr in range(2):
                pe.wait_ge(s["pn"], (g * 2) + (2 * GROUPS * p + pr + 1))
                pe.wait_ge(s["c_free"], c_t(p, g, pr) - (RING_C - 1))
                for q in range(4):
                    mm = pe.transpose(c_bank(pr)[:, q * P:(q + 1) * P], pw[:, pr, q * P:(q + 1) * P], ident[:])
                mm.then_inc(s["c_ready"], 1)

        def pe_s(pe, p, g):
            pe.wait_ge(s["wal"], load_of(p, g) * CK + CK)

            def part(pr, h, ks):
                col = (2 * pr + h) * P
                for k in ks:
                    if h == 0:
                        pe.wait_ge(s["mvl"], mv_m(p, g, CK + k + 1))
                    mm = three_passes(pe, c_bank(pr)[:, 256 * h:256 * (h + 1)],
                                      wah[:, k, col:col + P], wal[:, k, col:col + P],
                                      mh[:, k, :, col:col + P], ml[:, k, :, col:col + P], k == 0, k == CK - 1)
                return mm

            for pr in range(2):
                wait_bank(pe, "c_free", c_s(p, g, pr), RING_C)
                part(pr, 0, range(CK - 1))
            for pr in range(2):
                part(pr, 0, range(CK - 1, CK))
                part(pr, 1, range(CK)).then_inc(s["c_ready"], 1)

        def pe_v(pe, p, g, i):
            if i == 0:
                pe.wait_ge(s["xth"], PB * CK * (p + 1))
                pe.wait_ge(s["xtl"], PB * CK * (p + 1))
            for j in range(TJ):
                u = TJ * i + j
                wait_bank(pe, "a_free", a_v(p, g, u), RING_A)
                for k in range(CK):
                    if u == 0:
                        pe.wait_ge(s["wal"], load_of(p, g + GROUPS) * CK + (k + 1))
                    mm = three_passes(pe, a_bank(u)[:], xth[:, i, k, j * P:(j + 1) * P], xtl[:, i, k, j * P:(j + 1) * P],
                                      wah[:, k, :], wal[:, k, :], k == 0, k == CK - 1)
                mm.then_inc(s["a_ready"], 1)

        def pe_z(pe, p, g, i, h, tiles):
            u = HG * i + h
            if 0 in tiles:
                wait_bank(pe, "b_free", b_z(p, g, u), RING_B)
            for j in tiles:
                if h == 0:
                    pe.wait_ge(s["mvl"], mv_v(p, g, TJ * i + j + 1))
                    if i == 0:
                        pe.wait_ge(s["wbl"], load_of(p, g + GROUPS) * CK + (j + 1))
                mm = three_passes(pe, b_bank(u)[:], vh[:, j, h * P:(h + 1) * P], vl[:, j, h * P:(h + 1) * P],
                                  wbh[:, j, :], wbl[:, j, :], j == 0, j == TJ - 1)
            if TJ - 1 in tiles:
                mm.then_inc(s["b_ready"], 1)

        def pe_out(pe, p, g, i, h):
            if i == 0 and h == 0:
                pe.wait_ge(s["ptl"], g + (GROUPS * p + 1))
            u = HG * i + h
            pe.wait_ge(s["gzh"], b_z(p, g, u + 1))
            pe.wait_ge(s["b_free"], b_z(p, g, u + 1))
            pe.wait_ge(s["c_free"], c_out(p, g, u) - (RING_C - 1))
            q = (h % 2 * PB + i) * P
            mm = three_passes(pe, c_bank(u)[:], pth[:, h // 2, q:q + P], ptl[:, h // 2, q:q + P],
                              zh[:, h, :], zl[:, h, :], True, True)
            mm.then_inc(s["c_ready"], 1)

        def pe_values(pe, p, g, between=None):
            cut = (TJ - 1, Z1_EARLY)
            pe_v(pe, p, g, 0)
            if between:
                between()
            for i in range(PB):
                for h in range(2):
                    pe_z(pe, p, g, i, h, range(cut[h]))
                for h in range(2):
                    pe_z(pe, p, g, i, h, range(cut[h], TJ))
                for h in range(2, HG):
                    pe_z(pe, p, g, i, h, range(TJ))
                if i == 0:
                    pe_v(pe, p, g, 1)
                    for h in range(HG):
                        pe_out(pe, p, g, 0, h)
            for h in range(HG):
                pe_out(pe, p, g, 1, h)

        @block.tensor
        def _(pe):
            pe.wait_ge(s["ident"], 2)
            for p in range(PASSES):
                pe_norm(pe, p)
                pe_m(pe, p, 0)
                pe_s(pe, p, 0)
                with pe.Fori(1, GROUPS) as g:
                    pe_m(pe, p, g, lambda u: pe_t(pe, p, g - 1) if u == T_AFTER else None)
                    pe_s(pe, p, g)
                pe_values(pe, p, 0, lambda: pe_t(pe, p, GROUPS - 1))
                with pe.Fori(1, GROUPS) as g:
                    pe_values(pe, p, g)
            stage_b_pe(pe)

        def act_colsum(act, g):
            act.wait_ge(s["wqt_in"], 16 * (g + 1))
            for h in range(HG):
                act.activation(wqt[g][:, h, :], wqt[g][:, h, :], ACT.Copy,
                               accum_out=cs[:, HG * g + h:HG * g + h + 1]).then_inc(s["colsum"], 1)

        def act_norm(act, p):
            for i in range(PB):
                n = PB * TJ * p + TJ * i
                if i:
                    act.wait_ge(s["b_ready"], b_g(p, CK))
                elif p:
                    act.wait_ge(s["w_abs"], 1 + 3 * GROUPS)
                    act.wait_ge(s["c_ready"], c_s(p, 0, 0))
                for j in range(TJ):
                    act.wait_ge(s["xn"], n + j + 1)
                    act.activation(xh[:, j, :], xnf[i][:, j, :], ACT.Copy).then_inc(s["xh"], 1)
                    act.activation(ph[:, j, :], xnf[i][:, j, :], ACT.Copy, bias=SHIFT).then_inc(s["ph"], 1)
                for c in range(CK):
                    u = CK * i + c
                    act.wait_ge(s["a_ready"], a_xt(p, u) + 1)
                    act.activation(xth[:, i, c, :], a_bank(u)[:], ACT.Copy).then_inc(s["xth"], 1)
                for c in range(CK):
                    u = CK * i + c
                    if p == 0 and i == 0:
                        act_colsum(act, c)
                    act.wait_ge(s["b_ready"], b_g(p, u) + 1)
                    act.activation(gh[:, i, c, :], b_bank(u)[:], ACT.Copy).then_inc(s["gzh"], 1)

        def act_split_b(act, p, k, used, count):
            if used:
                act.wait_ge(s[used], count)
            act.wait_ge(s["raw_b"], load_of(p, k) * 16 + 16)
            for c in range(CK):
                act.activation(wbh[:, c, :], raw_b[:, c, :], ACT.Copy).then_inc(s["wbh"], 1)

        def act_split_a(act, p, k, used, count):
            if used:
                act.wait_ge(s[used], count)
            for c in range(CK):
                act.wait_ge(s["beta_add"], load_of(p, k) * CK + (c + 1))
                act.activation(wah[:, c, :], raw_a[:, c, :], ACT.Copy).then_inc(s["wah"], 1)

        def act_scores(act, p, g, first):
            start = p == 0 and first
            for u in range(8):
                i, c = u // CK, u % CK
                act.wait_ge(s["tmp"], mv_m(p, g, u + 1))
                if u == 0:
                    act.wait_ge(s["a_ready"], a_m(p, g, 1))
                act.activation(mh[:, c, i, :], tmp[:, u % 2, :], ACT.Copy).then_inc(s["mvh"], 1)
                if u == FIRST_SPLIT and start:
                    act_split_a(act, 0, 0, None, 0)
                if u == T_AFTER and not first:
                    act_pt(act, p, g - 1)
            act_split_b(act, p, g + 1, "a_ready", a_m(p, g, 8))
            for pr in range(2):
                act.wait_ge(s["nmx"], (g * 2) + (2 * GROUPS * p + pr + 1))
                for q in range(4):
                    e = act.activation(pw[:, pr, q * P:(q + 1) * P], c_bank(pr)[:, q * P:(q + 1) * P], ACT.Exp,
                                       bias=nmx[:, pr, q:q + 1], scale=SCALE_A, accum_out=rs[:, pr, q:q + 1])
                e.then_inc(s["c_free"], 1)
                if pr == 0:
                    act_split_a(act, p, g + 1, "c_ready", c_s(p, g, 2))

        def act_pt(act, p, g):
            for pr in range(2):
                act.wait_ge(s["c_ready"], c_t(p, g, pr) + 1)
                dst = ptf[:, g, pr, :] if isinstance(g, int) else ptf[:, bass.ds(g, 1), pr, :]
                src = c_bank(pr)[:] if isinstance(g, int) else c_bank(pr)[:].rearrange("p (a n) -> p a n", a=1)
                act.activation(dst, src, ACT.Copy).then_inc(s["c_free"], 1)

        def act_values(act, p, g, last):
            k = g + GROUPS
            first = isinstance(g, int) and g == 0
            if not first:
                act.wait_ge(s["c_ready"], c_out(p, g, 0))
            act.wait_ge(s["c_free"], C_TILES * p + 4 * GROUPS - (2 if first else 0))
            src = ptf[:, g] if isinstance(g, int) else ptf[:, bass.ds(g, 1)].rearrange("p a b n -> p (a b) n")
            act.activation(pth[:], src, ACT.Copy).then_inc(s["pth"], 1)

            def v_high(i):
                for j in range(TJ):
                    u = TJ * i + j
                    act.wait_ge(s["tmp"], mv_v(p, g, u + 1))
                    act.activation(vh[:, j, :], tmp[:, u % 2, :], ACT.Copy).then_inc(s["mvh"], 1)

            def z_high(i):
                for h in range(HG):
                    u = HG * i + h
                    act.wait_ge(s["b_ready"], b_z(p, g, u + 1))
                    act.activation(zh[:, h, :], b_bank(u)[:], ACT.Copy).then_inc(s["gzh"], 1)
                    if last and u == HG + 2:
                        act_prep(act, 0, 0)

            v_high(0)
            if first:
                act_pt(act, p, GROUPS - 1)
            z_high(0)
            v_high(1)
            if not last:
                act_split_a(act, *nxt(p, k), "a_ready", a_v(p, g, 8))
            z_high(1)
            if not last:
                act_split_b(act, *nxt(p, k), "b_ready", b_z(p, g, 8))
            if p == 0:
                act.wait_ge(s["w_raw"], g * 48 + 48)
                for w in range(3):
                    part = wsum[0:WP, w, bass.ds(g, 1)]
                    act.activation(wraw[:, w, :], wraw[:, w, :], ACT.Abs, accum_out=part).then_inc(s["w_abs"], 1)

        def nxt(p, k):
            if isinstance(k, int) and k == W_LOADS - 1:
                return p + 1, 0
            return p, k + 1

        @block.scalar
        def _(act):
            credit(act, "act")
            act_split_b(act, 0, 0, None, 0)
            for p in range(PASSES):
                act_norm(act, p)
                if p == 0:
                    act.wait_ge(s["w_pad"], 1)
                act_scores(act, p, 0, True)
                with act.Fori(1, GROUPS) as g:
                    act_scores(act, p, g, False)
                act_values(act, p, 0, False)
                with act.Fori(1, GROUPS - 1) as g:
                    act_values(act, p, g, False)
                act_values(act, p, GROUPS - 1, p == PASSES - 1)
            stage_b_act(act)

        chain = [0]

        def make_link(dve, name, chain):
            def link(ins):
                chain[0] += 1
                ins.then_inc(s[name], 1)
                dve.wait_ge(s[name], chain[0])
            return link

        def dve_stats(dve, link, src, part):
            if part < 2:
                for j in (2 * part, 2 * part + 1):
                    link(dve.bn_stats(bst[:, j, :], src[:, j, :]))
            else:
                for j in range(TJ):
                    link(dve.bn_aggr(mvar[:, j, :], bst[:, j, :]))
                link(dve.tensor_copy(nvar[:], mvar[:, :, 1]))
                newton_rsqrt(dve, link, rstd[:], ntmp[:], nvar[:])

        def dve_normalise(dve, link, p, i, part):
            n = PB * TJ * p + TJ * i
            if part == 0:
                dve.wait_ge(s["xn_in"], 16 * (PB * p + i + 1))
            if part < 3:
                dve_stats(dve, link, xnf[i], part)
            else:
                for j in range(TJ):
                    dve.tensor_scalar(xnf[i][:, j, :], xnf[i][:, j, :], mvar[:, j, 0:1], rstd[:, j:j + 1],
                                      ALU.subtract, ALU.mult).then_inc(s["xn"], 1)

        def dve_norm(dve, link, p):
            if p == 0:
                for part in range(4):
                    dve_normalise(dve, link, p, 0, part)
            for i in range(PB):
                n = PB * TJ * p + TJ * i
                dve.wait_ge(s["xn"], n + TJ)
                for j in range(TJ):
                    dve.wait_ge(s["ph"], n + j + 1)
                    dve.scalar_tensor_tensor(pl[:, j, :], xnf[i][:, j, :], SHIFT, ph[:, j, :].bitcast(F32),
                                             ALU.add, ALU.subtract).then_inc(s["pl"], 1)
                for c in range(CK):
                    u = CK * i + c
                    dve.wait_ge(s["xth"], PB * CK * p + u + 1)
                    dve.tensor_tensor(xtl[:, i, c, :], a_bank(u)[:], xth[:, i, c, :].bitcast(F32),
                                      ALU.subtract).then_inc(s["xtl"], 1)
                    dve.reduce_sum(shat[:, i, c:c + 1], a_bank(u)[:], axis=AX).then_inc(s["a_free"], 1)
                for c in range(CK):
                    u = CK * i + c
                    dve.wait_ge(s["gzh"], b_g(p, u) + 1)
                    dve.tensor_tensor(gl[:, i, c, :], b_bank(u)[:], gh[:, i, c, :].bitcast(F32),
                                      ALU.subtract).then_inc(s["b_free"], 1)
                    if p == 0 and i == 0:
                        for part in ((0, 1), (2,), (3,), ())[c]:
                            dve_normalise(dve, link, p, 1, part)
            dve.wait_ge(s["a_free"], a_xt(p, PB * CK))
            dve.tensor_scalar(shat[:], shat[:], SHIFT * T, None, ALU.add).then_inc(s["shat"], 1)
            dve.wait_ge(s["shat"], p + 1)

        def dve_beta(dve, link):
            dve.wait_ge(s["colsum"], NH)
            dve.wait_ge(s["bq_in"], 16)
            link(dve.scalar_tensor_tensor(betac[:], cs[:], -SHIFT, bqc[:], ALU.mult, ALU.add))
            dve.tensor_scalar(betac[:], betac[:], 1.0 / (C * SHIFT), None, ALU.mult).then_inc(s["beta_col"], 1)

        def dve_beta_add(dve, p, k):
            dve.wait_ge(s["raw_a"], load_of(p, k) * 32 + 32)
            for c in range(CK):
                dve.tensor_tensor(raw_a[:, c, :], raw_a[:, c, :], beta_bc[:], ALU.add).then_inc(s["beta_add"], 1)

        def dve_bo(dve, p):
            if p == 0:
                dve.wait_ge(s["bo_in"], 16)
            for i in range(PB):
                dve.wait_ge(s[f"x_in{i}"], 16 * (p + 1))
                for j in range(TJ):
                    dve.tensor_tensor(xacc[:, i, j, :], xacc[:, i, j, :], bo_bc[:], ALU.add).then_inc(s["xacc_bo"], 1)

        def dve_scores(dve, p, g, between=None):
            dve.wait_ge(s["bkv_in"], load_of(p, g) * 16 + 16)
            for u in range(8):
                i, c = u // CK, u % CK
                dve.wait_ge(s["a_ready"], a_m(p, g, u + 1))
                if not (p == 0 and isinstance(g, int) and u < 2):
                    dve.wait_ge(s["mvl"], mv_m(p, g, u - 1))
                dve.scalar_tensor_tensor(tmp[:, u % 2, :], bkv_bc[:], shat[:, i, c:c + 1], a_bank(u)[:],
                                         ALU.mult, ALU.add).then_inc(s["tmp"], 1)
                dve_release(dve, u, p, g, mv_m)
                if between:
                    between(u)
            dve.wait_ge(s["mvh"], mv_m(p, g, 8))
            dve.wait_ge(s["mvl"], mv_m(p, g, 7))
            dve.tensor_tensor(ml[:, CK - 1, PB - 1, :], tmp[:, 1, :], mh[:, CK - 1, PB - 1, :].bitcast(F32),
                              ALU.subtract).then_inc(s["mvl"], 1)
            dve_beta_add(dve, p, g + 1)
            for pr in range(2):
                n = (g * 2) + (2 * GROUPS * p + pr + 1)
                dve.wait_ge(s["c_ready"], c_s(p, g, pr) + 1)
                if p or not isinstance(g, int):
                    dve.wait_ge(s["c_free"], c_s(p, g, pr) - 3)
                dve.reduce_max(mx[:, pr, :], c_bank(pr)[:].rearrange("p (a n) -> p a n", n=P), axis=AX).then_inc(s["mx"], 1)
                dve.wait_ge(s["mx"], n)
                dve.tensor_scalar(nmx[:, pr, :], mx[:, pr, :], -SCALE_A, None, ALU.mult).then_inc(s["nmx"], 1)
            for pr in range(2):
                n = (g * 2) + (2 * GROUPS * p + pr + 1)
                dve.wait_ge(s["c_free"], c_s(p, g, pr) + 1)
                dve.reciprocal(rinv[:, pr, :], rs[:, pr, :]).then_inc(s["rinv"], 1)
                dve.wait_ge(s["rinv"], n)
                w = pw[:, pr, :].rearrange("p (a n) -> p a n", n=P)
                dve.tensor_tensor(w, w, rinv[:, pr, :].rearrange("p (a n) -> p a n", n=1).to_broadcast([P, 4, P]),
                                  ALU.mult).then_inc(s["pn"], 1)
        def dve_release(dve, u, p, g, mv):
            dve.wait_ge(s["tmp"], mv(p, g, u + 1))
            dve.sem_inc(s["a_free"], 1)

        def dve_values(dve, p, g, last, between=None):
            k = g + GROUPS
            dve.wait_ge(s["bkv_in"], load_of(p, k) * 16 + 16)

            def v_bias(i):
                for j in range(TJ):
                    u = TJ * i + j
                    dve.wait_ge(s["a_ready"], a_v(p, g, u + 1))
                    dve.wait_ge(s["mvl"], mv_v(p, g, u - 1))
                    dve.tensor_tensor(tmp[:, u % 2, :], a_bank(u)[:], bkv_bc[:], ALU.add).then_inc(s["tmp"], 1)
                    dve_release(dve, u, p, g, mv_v)

            def z_low(i, h):
                u = HG * i + h
                dve.wait_ge(s["gzh"], b_z(p, g, u + 1))
                dve.tensor_tensor(zl[:, h, :], b_bank(u)[:], zh[:, h, :].bitcast(F32),
                                  ALU.subtract).then_inc(s["b_free"], 1)
                if between:
                    between(u)

            def add_out(i, h):
                if i == 0 and h == 0:
                    dve.wait_ge(s["xacc_bo"], PB * TJ * (p + 1))
                u = HG * i + h
                dve.wait_ge(s["c_ready"], c_out(p, g, u + 1))
                dve.tensor_tensor(xacc[:, i, h, :], xacc[:, i, h, :], c_bank(u)[:], ALU.add).then_inc(s["c_free"], 1)

            v_bias(0)
            for h in range(HG):
                z_low(0, h)
            v_bias(1)
            for h in range(HG):
                add_out(0, h)
            if not last:
                dve_beta_add(dve, *nxt(p, k))
            for h in range(HG):
                z_low(1, h)
            for h in range(HG):
                add_out(1, h)

        def dve_weight_sums(dve):
            dve.wait_ge(s["w_abs"], 1 + 3 * GROUPS)
            dve.reduce_sum(wmean[:], wsum[:], axis=AX).then_inc(s["w_sum"], 1)

        def dve_weight_means(dve, link):
            dve.wait_ge(s["w_sum"], 2)
            link(dve.tensor_scalar(wmean[:], wthr[:, 0, :], 1.0 / (HID * C), None, ALU.mult))
            link(dve.tensor_scalar(wthr[:, 0, :], wmean[:], 0.5, None, ALU.mult))
            link(dve.tensor_scalar(wthr[:, 1, :], wmean[:], -0.5, None, ALU.mult))
            link(dve.tensor_tensor(wscale[:], wthr[:, 0, 0:1], wmean[:, 1:2], ALU.mult))

        def dve_ternary(dve, g, w):
            dve.wait_ge(s["w_raw"], g * 48 + (48 * GROUPS + 48))
            dve.wait_ge(s["w_q"], 1 + g * 3 + w)
            dve.tensor_scalar(wlow[:], wraw[:, w, :], wthr[0:WP, 1, w:w + 1], None, ALU.is_lt).then_inc(s["w_low"], 1)
            dve.wait_ge(s["w_low"], g * 3 + (w + 1))
            dve.scalar_tensor_tensor(wraw[:, w, :], wraw[:, w, :], wthr[0:WP, 0, w:w + 1], wlow[:],
                                     ALU.is_gt, ALU.subtract).then_inc(s["w_q"], 1)

        def dve_x1(dve, link, p, i, part):
            if part == 0:
                dve.wait_ge(s["c_free"], c_out(p, GROUPS - 1, HG * (i + 1)))
            if part < 3:
                dve_stats(dve, link, xacc[:, i], part)
            else:
                link(dve.tensor_copy(stat[:, i, :, 0], mvar[:, :, 0]))
                dve.tensor_scalar(stat[:, i, :, 1], rstd[:], SCALE_X, None, ALU.mult).then_inc(s["x1_ready"], 1)
                dve.wait_ge(s["x1_ready"], PB * p + i + 1)

        @block.vector
        def _(dve):
            credit(dve, "dve")
            link = make_link(dve, "link", chain)
            dve.memset(pw[0:1, 0, :], 0.0).then_inc(s["zero_beta"], 1)
            for p in range(PASSES):
                dve_norm(dve, link, p)
                if p == 0:
                    dve_beta(dve, link)
                    dve_scores(dve, p, 0, lambda u: dve_beta_add(dve, 0, 0) if u == FIRST_SPLIT else None)
                else:
                    dve_scores(dve, p, 0, lambda u: dve_x1(dve, link, p - 1, u // 4, u % 4))
                    dve_weight_means(dve, link)
                with dve.Fori(1, GROUPS) as g:
                    dve_scores(dve, p, g)
                dve_bo(dve, p)
                def ternary(u):
                    if p == 1 and TERNARY_AT <= u < TERNARY_AT + 3:
                        dve_ternary(dve, g, u - TERNARY_AT)

                with dve.Fori(0, GROUPS - 1) as g:
                    dve_values(dve, p, g, False, ternary)
                if p < PASSES - 1:
                    dve_values(dve, p, GROUPS - 1, False, lambda u: dve_normalise(dve, link, p + 1, u // 4, u % 4))
                    dve_weight_sums(dve)
                else:
                    def last_between(u):
                        if u >= HG:
                            dve_x1(dve, link, p, 0, u - HG)
                        elif u >= TERNARY_AT:
                            dve_ternary(dve, GROUPS - 1, u - TERNARY_AT)
                        if u == HG + 2:
                            dve_q(dve, 0, 0)
                    dve_values(dve, p, GROUPS - 1, True, last_between)
            stage_b_dve(dve, link)

        def pool_norm(pool, p):
            for i in range(PB):
                n = PB * TJ * p + TJ * i
                for j in range(TJ):
                    pool.wait_ge(s["xh"], n + j + 1)
                    pool.tensor_tensor(xl[:, j, :], xnf[i][:, j, :], xh[:, j, :].bitcast(F32), ALU.subtract).then_inc(s["xl"], 1)

        def pool_split(pool, which, p, k):
            high, low, raw = {"a": (wah, wal, raw_a), "b": (wbh, wbl, raw_b)}[which]
            for c in range(CK):
                pool.wait_ge(s[f"w{which}h"], load_of(p, k) * CK + (c + 1))
                pool.tensor_tensor(low[:, c, :], raw[:, c, :], high[:, c, :].bitcast(F32),
                                   ALU.subtract).then_inc(s[f"w{which}l"], 1)

        def pool_low(pool, dst, slot, index):
            pool.wait_ge(s["mvh"], index + 1)
            high, low = dst
            pool.tensor_tensor(low, tmp[:, slot, :], high.bitcast(F32), ALU.subtract).then_inc(s["mvl"], 1)

        def pool_scores(pool, p, g):
            for u in range(7):
                i, c = u // CK, u % CK
                pool_low(pool, (mh[:, c, i, :], ml[:, c, i, :]), u % 2, mv_m(p, g, u))
                if u == FIRST_SPLIT and p == 0 and isinstance(g, int):
                    pool_split(pool, "a", 0, 0)
            pool_split(pool, "b", p, g + 1)
            pool_split(pool, "a", p, g + 1)

        def pool_values(pool, p, g, last):
            k = g + GROUPS
            pool.wait_ge(s["pth"], g + (GROUPS * p + 1))
            src = ptf[:, g] if isinstance(g, int) else ptf[:, bass.ds(g, 1)].rearrange("p a b n -> p (a b) n")
            pool.tensor_tensor(ptl[:], src, pth[:].bitcast(F32), ALU.subtract).then_inc(s["ptl"], 1)
            for u in range(8):
                pool_low(pool, (vh[:, u % TJ, :], vl[:, u % TJ, :]), u % 2, mv_v(p, g, u))
            if not last:
                pool_split(pool, "a", *nxt(p, k))
                pool_split(pool, "b", *nxt(p, k))

        @block.gpsimd
        def _(pool):
            credit(pool, "pool")
            pool.memset(ident[:], 0.0).then_inc(s["ident"], 1)
            pool.wait_ge(s["ident"], 1)
            pool.affine_select(out=ident[:], in_=ident[:], compare_op=ALU.not_equal, fill=1.0, base=0,
                               pattern=[[-1, P]], channel_multiplier=1).then_inc(s["ident"], 1)
            pool.memset(wsum[:], 0.0).then_inc(s["w_pad"], 1)
            for p in range(PASSES):
                if p == 1:
                    pool.wait_ge(s["w_sum"], 1)
                    pool.partition_all_reduce(wthr[:, 0, :], wmean[:], P, bass.bass_isa.ReduceOp.add).then_inc(s["w_sum"], 1)
                if p == 0:
                    pool_split(pool, "b", 0, 0)
                pool_norm(pool, p)
                pool_scores(pool, p, 0)
                with pool.Fori(1, GROUPS) as g:
                    pool_scores(pool, p, g)
                with pool.Fori(0, GROUPS - 1) as g:
                    pool_values(pool, p, g, False)
                pool_values(pool, p, GROUPS - 1, p == PASSES - 1)
            stage_b_pool(pool)


def kernel(x, ctx_2048, L0_attn_Wq, L0_attn_bq, L0_attn_Wk, L0_attn_bk, L0_attn_Wv, L0_attn_bv, L0_attn_Wo, L0_attn_bo,
           L0_xattn_gamma, L0_ffn_w1, L0_ffn_w3, L0_ffn_w2):
    import numpy as np
    import concourse.bacc as bacc
    from concourse.bass_utils import run_bass_kernel_spmd

    D = np.asarray(L0_attn_Wq).shape[0]

    def by_group(w):
        return np.asarray(w).reshape(D, P, NH // GROUPS, GROUPS).transpose(3, 0, 2, 1).reshape(GROUPS, D, HG * P)

    def bias_by_group(b):
        return np.asarray(b).reshape(P, NH // GROUPS, GROUPS).transpose(2, 1, 0).reshape(GROUPS, HG * P)

    wq, wk, wv = by_group(L0_attn_Wq), by_group(L0_attn_Wk), by_group(L0_attn_Wv)
    wo = np.asarray(L0_attn_Wo).reshape(GROUPS, P, TJ, D).transpose(0, 2, 1, 3).reshape(GROUPS, T, D)
    arrays = {
        "x": x, "ctx": ctx_2048,
        "wa": np.concatenate([wq, wv]), "wb": np.concatenate([wk, wo]),
        "wq_t": wq.reshape(GROUPS, D, HG, P).transpose(0, 3, 2, 1),
        "bq_col": np.asarray(L0_attn_bq).reshape(P, HG, GROUPS).transpose(0, 2, 1).reshape(P, NH),
        "bkv": np.concatenate([bias_by_group(L0_attn_bk), bias_by_group(L0_attn_bv)]),
        "bo": L0_attn_bo, "gamma": np.asarray(L0_xattn_gamma).reshape(1, 1),
        "w1t": np.asarray(L0_ffn_w1).T, "w3t": np.asarray(L0_ffn_w3).T, "w2t": np.asarray(L0_ffn_w2).T,
    }
    arrays = {k: np.ascontiguousarray(v) for k, v in arrays.items()}
    nc = bacc.Bacc("TRN2", target_bir_lowering=False, num_devices=1)
    args = [nc.dram_tensor("in_" + k, v.shape, mybir.dt.from_np(v.dtype), kind="ExternalInput").ap() for k, v in arrays.items()]
    out = nc.dram_tensor("out_0", (B, T, C), F32, kind="ExternalOutput").ap()
    decoder_block(nc, *args, out)
    r = run_bass_kernel_spmd(nc, [{"in_" + k: v for k, v in arrays.items()}], core_ids=[0])
    return r.results[0]["out_0"]
```
